# Optimizing a Trainium2 kernel written in Bass

```python
import numpy as np
import jax
import jax.numpy as jnp

def _softmax(x, axis=-1):
    return jax.nn.softmax(x, axis=axis)

def _gelu(x):
    return jax.nn.gelu(x, approximate=True)

def _silu(x):
    return jax.nn.silu(x)

def _sigmoid(x):
    return jax.nn.sigmoid(x)

def _layernorm(x, axis=-1, eps=1e-05):
    m = jnp.mean(x, axis=axis, keepdims=True)
    v = jnp.var(x, axis=axis, keepdims=True)
    return (x - m) / jnp.sqrt(v + eps)

def _scatter_add(tgt, idx, src, axis=0):
    return tgt.at[idx].add(src)

def _segment_sum(src, seg, n):
    return jax.ops.segment_sum(src, seg, n)
kernel_name = 'mk_conv_preact_d4_conv_nchw384_r4_98ae3f'

def setup_inputs(seed: int=0):
    np.random.seed(seed)
    _w = jnp.asarray

    def _rec_inputs():
        import jax
        import jax.numpy as jnp
        _gk = jax.random.key(seed)
        x = -0.0002221 + 1 * jax.random.normal(jax.random.fold_in(_gk, 1), (16, 96, 16, 16), jnp.float32)
        return x
    x = _rec_inputs()

    def _L0_conv_setup():
        import jax, jax.numpy as jnp
        import numpy as np
        B, C, H, W = (16, 96, 16, 16)
        S, R, GR = (16, 8, 16)
        EPS = 1e-06

        def _ssm1d(x, a_logit, U, V, Win, bin_, Wg, bg, Wout, bout, Wskip, bskip, reverse):
            if reverse:
                x = x[:, ::-1]
            u = jnp.einsum('nld,sd->nls', x, Win) + bin_
            g = jax.nn.sigmoid(jnp.einsum('nld,sd->nls', x, Wg) + bg)
            a = jax.nn.sigmoid(a_logit)
            A = jnp.diag(a) + (U @ V.T).T
            gu = jnp.swapaxes(g * u, 0, 1)
            h0 = jnp.zeros((x.shape[0], a.shape[0]), x.dtype)

            def step(h, gu_t):
                h = h @ A + gu_t
                return (h, h)
            _, hs = jax.lax.scan(step, h0, gu)
            hs = jnp.swapaxes(hs, 0, 1)
            y = jnp.einsum('nls,ds->nld', hs, Wout) + bout + jnp.einsum('nld,ed->nle', x, Wskip) + bskip
            if reverse:
                y = y[:, ::-1]
            return y

        def _forward(x, rp, cp, g1_w, g1_b, g2_w, g2_b, norm_w, norm_b):
            Bx, Cx, Hx, Wx = x.shape
            rows = jnp.transpose(x, (0, 2, 3, 1)).reshape(Bx * Hx, Wx, Cx)
            cols = jnp.transpose(x, (0, 3, 2, 1)).reshape(Bx * Wx, Hx, Cx)
            yr = _ssm1d(rows, *rp, False) + _ssm1d(rows, *rp, True)
            yc = _ssm1d(cols, *cp, False) + _ssm1d(cols, *cp, True)
            yr = jnp.transpose(yr.reshape(Bx, Hx, Wx, Cx), (0, 3, 1, 2))
            yc = jnp.transpose(yc.reshape(Bx, Wx, Hx, Cx), (0, 3, 2, 1))
            y = (yr + yc) * 0.25
            mean = x.mean(axis=1, keepdims=True)
            var = ((x - mean) ** 2).mean(axis=1, keepdims=True)
            xn = (x - mean) / jnp.sqrt(var + EPS)
            xn = xn * norm_w[None, :, None, None] + norm_b[None, :, None, None]
            h1 = jax.nn.gelu(jnp.einsum('bchw,oc->bohw', xn, g1_w) + g1_b[None, :, None, None], approximate=False)
            g = jax.nn.sigmoid(jnp.einsum('bghw,cg->bchw', h1, g2_w) + g2_b[None, :, None, None])
            return g * y + (1.0 - g) * x
        key = jax.random.key(seed)
        ks = jax.random.split(key, 16)

        def rn(k, shape, s):
            return jax.random.normal(k, shape, dtype=jnp.float32) * s
        inp = {'x': jax.random.normal(ks[0], (B, C, H, W), dtype=jnp.float32)}
        i = 1
        for p in ('row', 'col'):
            inp[p + '_a_logit'] = jnp.zeros((S,), jnp.float32)
            inp[p + '_U'] = rn(ks[i], (S, R), 0.02)
            i += 1
            inp[p + '_V'] = rn(ks[i], (S, R), 0.02)
            i += 1
            inp[p + '_Win'] = rn(ks[i], (S, C), 1.0 / np.sqrt(C))
            i += 1
            inp[p + '_bin'] = jnp.zeros((S,), jnp.float32)
            inp[p + '_Wg'] = rn(ks[i], (S, C), 1.0 / np.sqrt(C))
            i += 1
            inp[p + '_bg'] = jnp.zeros((S,), jnp.float32)
            inp[p + '_Wout'] = rn(ks[i], (C, S), 1.0 / np.sqrt(S))
            i += 1
            inp[p + '_bout'] = jnp.zeros((C,), jnp.float32)
            inp[p + '_Wskip'] = rn(ks[i], (C, C), 1.0 / np.sqrt(C))
            i += 1
            inp[p + '_bskip'] = jnp.zeros((C,), jnp.float32)
        inp['g1_w'] = rn(ks[i], (GR, C), 1.0 / np.sqrt(C))
        i += 1
        inp['g1_b'] = jnp.zeros((GR,), jnp.float32)
        inp['g2_w'] = rn(ks[i], (C, GR), 1.0 / np.sqrt(GR))
        i += 1
        inp['g2_b'] = jnp.zeros((C,), jnp.float32)
        inp['norm_w'] = jnp.ones((C,), jnp.float32)
        inp['norm_b'] = jnpp = jnp.zeros((C,), jnp.float32)
        inp['norm_b'] = jnp.zeros((C,), jnp.float32)
        return inp
    _L0_conv_all = _L0_conv_setup()
    _L0_conv_in = {k: v for k, v in _L0_conv_all.items() if k in ('row_a_logit', 'row_U', 'row_V', 'row_Win', 'row_bin', 'row_Wg', 'row_bg', 'row_Wout', 'row_bout', 'row_Wskip', 'row_bskip', 'col_a_logit', 'col_U', 'col_V', 'col_Win', 'col_bin', 'col_Wg', 'col_bg', 'col_Wout', 'col_bout', 'col_Wskip', 'col_bskip', 'g1_w', 'g1_b', 'g2_w', 'g2_b', 'norm_w', 'norm_b')}
    del _L0_conv_all

    def _L1_conv_setup():
        import jax, jax.numpy as jnp
        import numpy as np
        K = 2
        BN_EPS = 1e-05
        key = jax.random.key(seed)
        ks = jax.random.split(key, 6)
        B, C, H, W = (16, 96, 28, 28)
        Cout = 96
        x = jax.random.normal(ks[0], (B, C, H, W), dtype=jnp.float32)
        conv_w = jax.random.normal(ks[1], (Cout, 2 * C), dtype=jnp.float32) * (1.0 / np.sqrt(2 * C))
        conv_b = jax.random.normal(ks[2], (Cout,), dtype=jnp.float32) * 0.01
        bn_gamma = jnp.ones((Cout,), dtype=jnp.float32) + 0.1 * jax.random.normal(ks[3], (Cout,), dtype=jnp.float32)
        bn_beta = 0.1 * jax.random.normal(ks[4], (Cout,), dtype=jnp.float32)
        bn_mean = 0.1 * jax.random.normal(ks[5], (Cout,), dtype=jnp.float32)
        bn_var = jnp.ones((Cout,), dtype=jnp.float32) * 0.9
        return {'x': x, 'conv_w': conv_w, 'conv_b': conv_b, 'bn_gamma': bn_gamma, 'bn_beta': bn_beta, 'bn_mean': bn_mean, 'bn_var': bn_var}
    _L1_conv_all = _L1_conv_setup()
    _L1_conv_in = {k: v for k, v in _L1_conv_all.items() if k in ('conv_w', 'conv_b', 'bn_gamma', 'bn_beta', 'bn_mean', 'bn_var')}
    del _L1_conv_all

    def _L2_conv_setup():
        import jax, jax.numpy as jnp
        import numpy as np
        from jax import lax
        PLANES = 96
        N_POINTS = 4
        KERNEL_SIZE = 11
        INIT_RADIUS = 2.0 * (2.0 / KERNEL_SIZE)

        def _make_kernels(weight_coord, radius, weights):
            K = KERNEL_SIZE
            lin = jnp.linspace(-1.0, 1.0, K)
            gy, gx = jnp.meshgrid(lin, lin, indexing='ij')
            kernel_coord = jnp.stack([gy, gx], axis=0).reshape(2, K * K)
            diff = weight_coord[:, :, None, :] - kernel_coord.T[None, None, :, :]
            diff = jnp.transpose(diff, (0, 1, 3, 2)).reshape(1, N_POINTS, 2, K, K)
            d = jax.nn.relu(1.0 - jnp.abs(diff).sum(axis=2) / radius)
            kernels = jnp.matmul(weights, d.reshape(1, N_POINTS, K * K)).reshape(PLANES, K, K)
            kernels = jnp.flip(jnp.transpose(kernels, (0, 2, 1)), axis=1)
            return kernels
        key = jax.random.key(seed)
        k1, k2, k3 = jax.random.split(key, 3)
        x = jax.random.normal(k1, (16, PLANES, 16, 16), dtype=jnp.float32)
        weight_coord = jnp.clip(0.2 * jax.random.normal(k2, (1, N_POINTS, 2), dtype=jnp.float32), -1.0, 1.0)
        radius = jnp.full((1, N_POINTS, 1, 1), INIT_RADIUS, dtype=jnp.float32)
        weights = 0.02 * jax.random.normal(k3, (1, PLANES, N_POINTS), dtype=jnp.float32)
        return {'x': x, 'weight_coord': weight_coord, 'radius': radius, 'weights': weights}
    _L2_conv_all = _L2_conv_setup()
    _L2_conv_in = {k: v for k, v in _L2_conv_all.items() if k in ('weight_coord', 'radius', 'weights')}
    del _L2_conv_all

    def _L3_conv_setup():
        import jax, jax.numpy as jnp
        import numpy as np
        B, DIM, H, W = (2, 96, 64, 64)
        HID = DIM * 1
        P = 8
        key = jax.random.key(seed)
        k0, k1, k2, k3, k4 = jax.random.split(key, 5)
        x = jax.random.normal(k0, (B, DIM, H, W), jnp.float32)
        fft_filter = jax.random.normal(k1, (HID, P, P // 2 + 1), jnp.float32)
        w_in = jax.random.normal(k2, (HID, DIM), jnp.float32) * (1.0 / np.sqrt(DIM))
        w_dw = jax.random.normal(k3, (HID, 1, 3, 3), jnp.float32) * (1.0 / 3.0)
        w_out = jax.random.normal(k4, (DIM, HID // 2), jnp.float32) * (1.0 / np.sqrt(HID // 2))
        return {'x': x, 'fft_filter': fft_filter, 'w_in': w_in, 'w_dw': w_dw, 'w_out': w_out}
    _L3_conv_all = _L3_conv_setup()
    _L3_conv_in = {k: v for k, v in _L3_conv_all.items() if k in ('fft_filter', 'w_in', 'w_dw', 'w_out')}
    del _L3_conv_all
    return {'x': x, 'L0_conv_row_a_logit': _L0_conv_in['row_a_logit'], 'L0_conv_row_U': _L0_conv_in['row_U'], 'L0_conv_row_V': _L0_conv_in['row_V'], 'L0_conv_row_Win': _L0_conv_in['row_Win'], 'L0_conv_row_bin': _L0_conv_in['row_bin'], 'L0_conv_row_Wg': _L0_conv_in['row_Wg'], 'L0_conv_row_bg': _L0_conv_in['row_bg'], 'L0_conv_row_Wout': _L0_conv_in['row_Wout'], 'L0_conv_row_bout': _L0_conv_in['row_bout'], 'L0_conv_row_Wskip': _L0_conv_in['row_Wskip'], 'L0_conv_row_bskip': _L0_conv_in['row_bskip'], 'L0_conv_col_a_logit': _L0_conv_in['col_a_logit'], 'L0_conv_col_U': _L0_conv_in['col_U'], 'L0_conv_col_V': _L0_conv_in['col_V'], 'L0_conv_col_Win': _L0_conv_in['col_Win'], 'L0_conv_col_bin': _L0_conv_in['col_bin'], 'L0_conv_col_Wg': _L0_conv_in['col_Wg'], 'L0_conv_col_bg': _L0_conv_in['col_bg'], 'L0_conv_col_Wout': _L0_conv_in['col_Wout'], 'L0_conv_col_bout': _L0_conv_in['col_bout'], 'L0_conv_col_Wskip': _L0_conv_in['col_Wskip'], 'L0_conv_col_bskip': _L0_conv_in['col_bskip'], 'L0_conv_g1_w': _L0_conv_in['g1_w'], 'L0_conv_g1_b': _L0_conv_in['g1_b'], 'L0_conv_g2_w': _L0_conv_in['g2_w'], 'L0_conv_g2_b': _L0_conv_in['g2_b'], 'L0_conv_norm_w': _L0_conv_in['norm_w'], 'L0_conv_norm_b': _L0_conv_in['norm_b'], 'L1_conv_conv_w': _L1_conv_in['conv_w'], 'L1_conv_conv_b': _L1_conv_in['conv_b'], 'L1_conv_bn_gamma': _L1_conv_in['bn_gamma'], 'L1_conv_bn_beta': _L1_conv_in['bn_beta'], 'L1_conv_bn_mean': _L1_conv_in['bn_mean'], 'L1_conv_bn_var': _L1_conv_in['bn_var'], 'L2_conv_weight_coord': _L2_conv_in['weight_coord'], 'L2_conv_radius': _L2_conv_in['radius'], 'L2_conv_weights': _L2_conv_in['weights'], 'L3_conv_fft_filter': _L3_conv_in['fft_filter'], 'L3_conv_w_in': _L3_conv_in['w_in'], 'L3_conv_w_dw': _L3_conv_in['w_dw'], 'L3_conv_w_out': _L3_conv_in['w_out']}

def reference(x, L0_conv_row_a_logit, L0_conv_row_U, L0_conv_row_V, L0_conv_row_Win, L0_conv_row_bin, L0_conv_row_Wg, L0_conv_row_bg, L0_conv_row_Wout, L0_conv_row_bout, L0_conv_row_Wskip, L0_conv_row_bskip, L0_conv_col_a_logit, L0_conv_col_U, L0_conv_col_V, L0_conv_col_Win, L0_conv_col_bin, L0_conv_col_Wg, L0_conv_col_bg, L0_conv_col_Wout, L0_conv_col_bout, L0_conv_col_Wskip, L0_conv_col_bskip, L0_conv_g1_w, L0_conv_g1_b, L0_conv_g2_w, L0_conv_g2_b, L0_conv_norm_w, L0_conv_norm_b, L1_conv_conv_w, L1_conv_conv_b, L1_conv_bn_gamma, L1_conv_bn_beta, L1_conv_bn_mean, L1_conv_bn_var, L2_conv_weight_coord, L2_conv_radius, L2_conv_weights, L3_conv_fft_filter, L3_conv_w_in, L3_conv_w_dw, L3_conv_w_out):
    import jax
    import jax.numpy as jnp

    def _L0_conv_ref(x, row_a_logit, row_U, row_V, row_Win, row_bin, row_Wg, row_bg, row_Wout, row_bout, row_Wskip, row_bskip, col_a_logit, col_U, col_V, col_Win, col_bin, col_Wg, col_bg, col_Wout, col_bout, col_Wskip, col_bskip, g1_w, g1_b, g2_w, g2_b, norm_w, norm_b):
        import jax, jax.numpy as jnp
        import numpy as np
        B, C, H, W = (16, 96, 16, 16)
        S, R, GR = (16, 8, 16)
        EPS = 1e-06

        def _ssm1d(x, a_logit, U, V, Win, bin_, Wg, bg, Wout, bout, Wskip, bskip, reverse):
            if reverse:
                x = x[:, ::-1]
            u = jnp.einsum('nld,sd->nls', x, Win) + bin_
            g = jax.nn.sigmoid(jnp.einsum('nld,sd->nls', x, Wg) + bg)
            a = jax.nn.sigmoid(a_logit)
            A = jnp.diag(a) + (U @ V.T).T
            gu = jnp.swapaxes(g * u, 0, 1)
            h0 = jnp.zeros((x.shape[0], a.shape[0]), x.dtype)

            def step(h, gu_t):
                h = h @ A + gu_t
                return (h, h)
            _, hs = jax.lax.scan(step, h0, gu)
            hs = jnp.swapaxes(hs, 0, 1)
            y = jnp.einsum('nls,ds->nld', hs, Wout) + bout + jnp.einsum('nld,ed->nle', x, Wskip) + bskip
            if reverse:
                y = y[:, ::-1]
            return y

        def _forward(x, rp, cp, g1_w, g1_b, g2_w, g2_b, norm_w, norm_b):
            Bx, Cx, Hx, Wx = x.shape
            rows = jnp.transpose(x, (0, 2, 3, 1)).reshape(Bx * Hx, Wx, Cx)
            cols = jnp.transpose(x, (0, 3, 2, 1)).reshape(Bx * Wx, Hx, Cx)
            yr = _ssm1d(rows, *rp, False) + _ssm1d(rows, *rp, True)
            yc = _ssm1d(cols, *cp, False) + _ssm1d(cols, *cp, True)
            yr = jnp.transpose(yr.reshape(Bx, Hx, Wx, Cx), (0, 3, 1, 2))
            yc = jnp.transpose(yc.reshape(Bx, Wx, Hx, Cx), (0, 3, 2, 1))
            y = (yr + yc) * 0.25
            mean = x.mean(axis=1, keepdims=True)
            var = ((x - mean) ** 2).mean(axis=1, keepdims=True)
            xn = (x - mean) / jnp.sqrt(var + EPS)
            xn = xn * norm_w[None, :, None, None] + norm_b[None, :, None, None]
            h1 = jax.nn.gelu(jnp.einsum('bchw,oc->bohw', xn, g1_w) + g1_b[None, :, None, None], approximate=False)
            g = jax.nn.sigmoid(jnp.einsum('bghw,cg->bchw', h1, g2_w) + g2_b[None, :, None, None])
            return g * y + (1.0 - g) * x
        rp = (row_a_logit, row_U, row_V, row_Win, row_bin, row_Wg, row_bg, row_Wout, row_bout, row_Wskip, row_bskip)
        cp = (col_a_logit, col_U, col_V, col_Win, col_bin, col_Wg, col_bg, col_Wout, col_bout, col_Wskip, col_bskip)
        return _forward(x, rp, cp, g1_w, g1_b, g2_w, g2_b, norm_w, norm_b)

    def _L1_conv_ref(x, conv_w, conv_b, bn_gamma, bn_beta, bn_mean, bn_var):
        import jax, jax.numpy as jnp
        import numpy as np
        K = 2
        BN_EPS = 1e-05
        x_j = jnp.zeros_like(x)
        for shift, axis in ((K, 2), (-K, 2), (K, 3), (-K, 3)):
            x_j = jnp.maximum(x_j, jnp.roll(x, shift, axis=axis) - x)
        y = jnp.concatenate([x, x_j], axis=1)
        h = jnp.einsum('bchw,oc->bohw', y, conv_w) + conv_b[None, :, None, None]
        inv = jax.lax.rsqrt(bn_var + BN_EPS)
        h = (h - bn_mean[None, :, None, None]) * (bn_gamma * inv)[None, :, None, None] + bn_beta[None, :, None, None]
        return jax.nn.gelu(h, approximate=False)

    def _L2_conv_ref(x, weight_coord, radius, weights):
        import jax, jax.numpy as jnp
        import numpy as np
        from jax import lax
        PLANES = 96
        N_POINTS = 4
        KERNEL_SIZE = 11
        INIT_RADIUS = 2.0 * (2.0 / KERNEL_SIZE)

        def _make_kernels(weight_coord, radius, weights):
            K = KERNEL_SIZE
            lin = jnp.linspace(-1.0, 1.0, K)
            gy, gx = jnp.meshgrid(lin, lin, indexing='ij')
            kernel_coord = jnp.stack([gy, gx], axis=0).reshape(2, K * K)
            diff = weight_coord[:, :, None, :] - kernel_coord.T[None, None, :, :]
            diff = jnp.transpose(diff, (0, 1, 3, 2)).reshape(1, N_POINTS, 2, K, K)
            d = jax.nn.relu(1.0 - jnp.abs(diff).sum(axis=2) / radius)
            kernels = jnp.matmul(weights, d.reshape(1, N_POINTS, K * K)).reshape(PLANES, K, K)
            kernels = jnp.flip(jnp.transpose(kernels, (0, 2, 1)), axis=1)
            return kernels
        kernels = _make_kernels(weight_coord, radius, weights)
        pad = KERNEL_SIZE // 2
        out = lax.conv_general_dilated(x, kernels[:, None, :, :], window_strides=(1, 1), padding=[(pad, pad), (pad, pad)], dimension_numbers=('NCHW', 'OIHW', 'NCHW'), feature_group_count=PLANES)
        return out

    def _L3_conv_ref(x, fft_filter, w_in, w_dw, w_out):
        import jax, jax.numpy as jnp
        import numpy as np
        B, DIM, H, W = (2, 96, 64, 64)
        HID = DIM * 1
        P = 8
        b, c, h, w = x.shape
        hid = w_in.shape[0]
        hb, wb = (h // P, w // P)
        t = jnp.einsum('bchw,oc->bohw', x, w_in)
        tp = t.reshape(b, hid, hb, P, wb, P)
        tf = jnp.fft.rfft2(tp, axes=(3, 5))
        tf = tf * fft_filter[None, :, None, :, None, :]
        tp = jnp.fft.irfft2(tf, s=(P, P), axes=(3, 5))
        t = tp.reshape(b, hid, h, w)
        t = jax.lax.conv_general_dilated(t, w_dw, window_strides=(1, 1), padding='SAME', feature_group_count=hid, dimension_numbers=('NCHW', 'OIHW', 'NCHW'))
        x1, x2 = (t[:, :hid // 2], t[:, hid // 2:])
        g = jax.nn.gelu(x1, approximate=False) * x2
        return jnp.einsum('bchw,oc->bohw', g, w_out)

    def _gn(v, G=32, eps=1e-05):
        B_, C_, H_, W_ = v.shape
        g = v.reshape(B_, G, C_ // G, H_, W_)
        m = jnp.mean(g, axis=(2, 3, 4), keepdims=True)
        s = jnp.var(g, axis=(2, 3, 4), keepdims=True)
        return ((g - m) / jnp.sqrt(s + eps)).reshape(v.shape)

    def _ln_c(v, eps=1e-06):
        m = jnp.mean(v, axis=1, keepdims=True)
        s = jnp.var(v, axis=1, keepdims=True)
        return (v - m) / jnp.sqrt(s + eps)

    def _ln_t(v, eps=1e-05):
        m = jnp.mean(v, axis=-1, keepdims=True)
        s = jnp.var(v, axis=-1, keepdims=True)
        return (v - m) / jnp.sqrt(s + eps)

    def _to_tokens(v):
        B_, C_, H_, W_ = v.shape
        return v.reshape(B_, C_, H_ * W_).transpose(0, 2, 1)

    def _from_tokens(t, like):
        B_, C_, H_, W_ = like.shape
        return t.transpose(0, 2, 1).reshape(B_, C_, H_, W_)
    x = x + _L0_conv_ref(_gn(x), L0_conv_row_a_logit, L0_conv_row_U, L0_conv_row_V, L0_conv_row_Win, L0_conv_row_bin, L0_conv_row_Wg, L0_conv_row_bg, L0_conv_row_Wout, L0_conv_row_bout, L0_conv_row_Wskip, L0_conv_row_bskip, L0_conv_col_a_logit, L0_conv_col_U, L0_conv_col_V, L0_conv_col_Win, L0_conv_col_bin, L0_conv_col_Wg, L0_conv_col_bg, L0_conv_col_Wout, L0_conv_col_bout, L0_conv_col_Wskip, L0_conv_col_bskip, L0_conv_g1_w, L0_conv_g1_b, L0_conv_g2_w, L0_conv_g2_b, L0_conv_norm_w, L0_conv_norm_b)
    x = x + _L1_conv_ref(_gn(x), L1_conv_conv_w, L1_conv_conv_b, L1_conv_bn_gamma, L1_conv_bn_beta, L1_conv_bn_mean, L1_conv_bn_var)
    x = x + _L2_conv_ref(_gn(x), L2_conv_weight_coord, L2_conv_radius, L2_conv_weights)
    x = x + _L3_conv_ref(_gn(x), L3_conv_fft_filter, L3_conv_w_in, L3_conv_w_dw, L3_conv_w_out)
    return x

_drawn_inputs = setup_inputs


def setup_inputs(seed=0):
    import zlib

    import numpy as np

    out = dict(_drawn_inputs(seed))
    spreads = {'L0_conv_row_a_logit': (0.0, 0.8),
     'L0_conv_row_bin': (0.0, 0.421),
     'L0_conv_row_bg': (0.0, 2.0),
     'L0_conv_row_bout': (0.0, 0.514),
     'L0_conv_row_bskip': (0.0, 0.54),
     'L0_conv_col_a_logit': (0.0, 0.8),
     'L0_conv_col_bin': (0.0, 0.58),
     'L0_conv_col_bg': (0.0, 0.8),
     'L0_conv_col_bout': (0.0, 0.596),
     'L0_conv_col_bskip': (0.0, 0.513),
     'L0_conv_g1_b': (0.0, 0.639),
     'L0_conv_g2_b': (0.0, 0.419),
     'L0_conv_norm_w': (1.0, 0.6),
     'L0_conv_norm_b': (0.0, 0.53),
     'L1_conv_bn_var': (0.8999999761581421, 0.2),
     'L2_conv_radius': (0.3636363744735718, 0.6)}
    factors = {'L0_conv_row_U': 8.0,
     'L0_conv_row_V': 8.0,
     'L0_conv_col_U': 8.0,
     'L0_conv_col_V': 8.0,
     'L1_conv_conv_b': 8.0,
     'L2_conv_weight_coord': 2.738}
    for name, (base, spread) in spreads.items():
        noise = np.random.default_rng([zlib.crc32(name.encode()), seed]).standard_normal(out[name].shape)
        drawn = base * np.exp(spread * noise) if base else spread * noise
        out[name] = jnp.asarray(drawn.astype(out[name].dtype))
    for name, factor in factors.items():
        out[name] = (out[name] * factor).astype(out[name].dtype)
    return out
```

```python
import numpy as np
import concourse.bass as bass
from concourse import mybir
from contextlib import ExitStack

B, C, H, W = 16, 96, 16, 16
S, R, GR = 16, 8, 16
NP = 2
PAIRS = B // NP
PIX = H * W
N = NP * PIX
HALF = PIX // 2
LN = H * NP
K2, PAD2, NPT = 11, 5, 4
P8 = 8
NF = P8 * (P8 // 2 + 1)
HID2 = C // 2
MID = 64
CP = MID + HID2
HP = H + 2
ROWS = NP * HP - 2
WIN = 3 * P8
BIG = 1e30
GN_EPS, LN_EPS, BN_EPS = 1e-5, 1e-6, 1e-5


STEPS = PAIRS + 3
FILL = 4
SETUP_DVE_A, SETUP_DVE_STRIP, SETUP_DVE_GN1, SETUP_DVE_ALL = 3, 14, 15, 38


def active(step):
    return (step < PAIRS, 1 <= step < PAIRS + 1, 2 <= step < PAIRS + 2, 3 <= step < STEPS, 3 <= step < STEPS)


def gn_range(step):
    on = [b for b, there in enumerate(active(step)[:3]) if there]
    return (on[0], on[-1] + 1) if on else None


def weight_layout():
    cols, at = {}, 0
    for name, n in [("proj", 64), ("ln", GR + 1), ("group", C), ("ones", C), ("g1", GR), ("nw", 1), ("nb", 1), ("g1b", GR),
                    ("bin", 1), ("bg", 1), ("alog", 1), ("vt", 32), ("ut", 32), ("id32", 32), ("g2", C), ("g2b", 1),
                    ("skr", C), ("skc", C), ("halfid", C), ("dlhs", C), ("dbias", 4),
                    ("w1", C), ("w2", C), ("cb", 1), ("gamma", 1), ("beta", 1), ("mean", 1), ("var", 1),
                    ("wc", 2 * NPT), ("rad", NPT), ("dx", W), ("bigx", W), ("dy", WIN), ("oney", WIN), ("wb", NPT * C),
                    ("win3", C), ("wout3", C), ("wdw", 9), ("filt", C), ("expand", 128), ("dft", 128), ("idft", 128),
                    ("ident", 128), ("mhalf", 16)]:
        cols[name] = (at, n)
        at += n
    return cols, at


def shape_constants():
    c = {}
    c["group"] = np.kron(np.eye(32), np.ones((3, 3))) / 6.0
    c["ones"] = np.full((C, C), 1.0 / C)
    c["halfid"] = 0.5 * np.eye(C)
    c["id32"] = np.eye(32)
    c["ident"] = np.eye(128)
    c["mhalf"] = np.full((128, 16), -0.5)
    yl, xi = np.divmod(np.arange(128), W)
    xo, q = np.arange(W), np.arange(-P8, 2 * P8)
    dx, dy = xi[:, None] - xo[None], yl[:, None] - q[None]
    c["dx"], c["dy"] = dx / PAD2, dy / PAD2
    c["bigx"] = np.where(np.abs(dx) <= PAD2, 0.0, BIG)
    c["oney"] = np.where(np.abs(dy) <= PAD2, 1.0, 1.0 - BIG)
    y, x = np.mgrid[0:P8, 0:P8]
    basis, expand = [], []
    for kx in range(P8 // 2 + 1):
        for ky in range(P8):
            own = np.zeros(NF)
            if kx in (0, P8 // 2):
                if ky > P8 // 2:
                    continue
                own[ky * 5 + kx] += 0.5
                own[(P8 - ky) % P8 * 5 + kx] += 0.5
            else:
                own[ky * 5 + kx] = 1.0
            angle = 2 * np.pi * (ky * y + kx * x) / P8
            if kx in (0, P8 // 2) and ky in (0, P8 // 2):
                basis.append(np.cos(angle) / P8)
                expand.append(own)
            else:
                basis += [np.sqrt(2) / P8 * np.cos(angle), np.sqrt(2) / P8 * np.sin(angle)]
                expand += [own, own]
    basis = np.array(basis)
    dft = np.zeros((P8, 2, P8, 2, 64))
    for b in range(2):
        dft[:, b, :, b, :] = basis.transpose(1, 2, 0)
    c["dft"] = dft.reshape(128, 128)
    c["idft"] = c["dft"].T
    c["expand"] = np.tile(np.array(expand).T, (1, 2))
    return c


def build(nc, x, wts, out):
    F32 = mybir.dt.float32
    ALU = mybir.AluOpType
    ACT = mybir.ActivationFunctionType
    AX = mybir.AxisListType
    cols, NW = weight_layout()

    ctx = ExitStack()
    with ctx:
        def sb(name, shape):
            return ctx.enter_context(nc.sbuf_tensor(name, shape, F32))

        def sem(name):
            return ctx.enter_context(nc.semaphore(name))

        wt = sb("weights", [128, NW])

        def w(name, p0=0, p1=128):
            at, n = cols[name]
            return wt[p0:p1, at:at + n]

        x0, x1, x2, x3 = (sb(f"x{i}", [C, N]) for i in range(4))
        x2_late, x_out, x0v0 = sb("x2_late", [C, N]), sb("x_out", [C, N]), sb("x0v0", [C, N])
        v_hs = sb("v_hs", [128, N])
        v0 = v_hs[0:C, :]
        v1, v2, v3 = (sb(f"v{i}", [C, N]) for i in range(1, 4))
        xs, vs = [x0, x1, x2, x3], [v0, v1, v2, v3]
        stats = sb("stats", [C, 4, NP, 6])
        halves = sb("halves", [C, 4, NP, 2])
        squares = sb("squares", [C, 4, NP, 2])
        moments = sb("moments", [C, 2, 4, NP])
        msq = sb("msq", [C, 4, NP])
        gvar = sb("gvar", [C, 4, NP])
        rstd = sb("rstd", [C, 4, NP])
        v0sq = sb("v0sq", [C, N])
        tanh_g, u_half = sb("tanh_g", [32, N]), sb("u_half", [32, N])
        ln_msq, ln_var, ln_rstd = (sb(n, [128, 2 * NP]) for n in ("ln_msq", "ln_var", "ln_rstd"))
        gu_col = sb("gu_col", [32, N])
        gu_row = sb("gu_row", [32, N])
        seq = sb("seq", [128, 2, 2, LN])
        hs = sb("hs", [128, 4 * LN])
        hs_row = sb("hs_row", [128, N])
        h_scaled, h_in, h1_pix = (sb(n, [128, 2 * NP, GR]) for n in ("h_scaled", "h_in", "h1_pix"))
        h1 = sb("h1", [GR, N])
        tanh_gate, d_half, gated = sb("tanh_gate", [C, N]), sb("d_half", [C, N]), sb("gated", [C, N])
        max_v1, max_v2, max_h, max_all = (sb(f"max{i}", [C, N]) for i in range(4))
        gelu1 = sb("gelu1", [C, N])
        bumps = sb("bumps", [128, NPT, WIN, W])
        xw = sb("xw", [128, NPT, 2, NP, C])
        y_pix = sb("y_pix", [128, 2, NP, C])
        t_pix = sb("t_pix", [128, 2 * NP, C])
        filt = sb("filt_spec", [128, C])
        spec = sb("spec", [128, 2 * NP, CP])
        tpad = sb("tpad", [CP, NP, HP, HP])
        conv = sb("conv", [CP, ROWS, W])
        gelu3, prod3 = sb("gelu3", [CP, N]), sb("prod3", [CP, N])
        gn1, hbias = sb("gn1", [C, GR]), sb("hbias", [128, GR])
        dlhs = w("dlhs")
        dsum, dbias = sb("dsum", [C, C]), sb("dbias_half", [C, 1])
        w12, bnv, bnr, bns, bnd, bnb = sb("w12", [C, C]), *(sb(f"bn{i}", [C, 1]) for i in range(5))
        sig_a = sb("sig_a", [32, 2])
        pw_a, pw_b = sb("pw_a", [32, 15, 32]), sb("pw_b", [32, 8, 32])
        strip = sb("strip", [32, 31, S])
        lines = sb("lines", [128, 2, 2, 256])
        toep = sb("toep", [128, 2, 2, 256])
        rinv, nrinv = sb("rinv", [128, NPT]), sb("nrinv", [128, NPT])
        axd, ax = sb("axd", [128, NPT, W]), sb("ax", [128, NPT, W])
        ayd, ay = sb("ayd", [128, NPT, WIN]), sb("ay", [128, NPT, WIN])
        axa, aya = sb("axa", [128, NPT, W]), sb("aya", [128, NPT, WIN])
        graw = sb("graw", [128, NPT, WIN, W])

        bank = [ctx.enter_context(nc.psum_tensor(f"bank{i}", [128, 512], F32)) for i in range(8)]
        p_gn = bank[0]
        p_proj, p_d = bank[1], bank[1]
        p_ln, p_toep = bank[2], bank[2]
        p_h, p_ssq = p_ln[:, 0:2 * NP * (GR + 1)].rearrange("p (a b) -> p a b", a=2 * NP), p_ln[:, 128:128 + 2 * NP]
        p_l1, p_h1, p_gate = bank[3], bank[3], bank[3]
        p_conv, p_xt = bank[4], bank[4]
        p_back, p_spec = bank[5], bank[5]
        p_t, p_inv = bank[6], bank[6]
        p_out = bank[7]

        names = """weights_in x_loaded gn_stats gn_sq gn_e2 gn_group gn_moments gn_msq gn_var gn_rstd v_ready
        gn3_stats gn3_sq gn3_e2 gn3_group gn3_moments gn3_msq gn3_var gn3_rstd v3_ready
        proj_done v0sq_done ssq_done proj_read gu_done gu_row_done seq_loaded toep_done hs_read hs_loaded hs_ready
        ln_msq_done ln_var_done ln_rstd_done h_scaled_done h_in_done h1_pix_done h1_back_done h1_done gate_done tanh_gate_done d_done d_read gated_done x0v0_done x1_done
        vert1_done vert2_done horiz_done max_done l1_done gelu1_done x2_done x2_late_done
        xt_done xw_done conv2_done y_pix_done back_done x3_done
        t_done t_pix_done spec_done spec_ready inv_done tpad_done tap_done gelu3_done prod3_done out_done x_out_done stored
        setup_pe setup_dve setup_act setup_pool lines_loaded toep_ready""".split()
        s = {n: sem(n) for n in names}

        def after(eng, name, count):
            if not isinstance(count, int) or count > 0:
                eng.wait_ge(s[name], count)

        def img(t, p0=0, p1=None):
            return t[p0:p1, :].rearrange("p (i h w) -> p i h w", i=NP, h=H)

        block = ctx.enter_context(nc.Block())

        @block.sync
        def _(sp):
            sp.dma_start(wt[:, :], wts).then_inc(s["weights_in"], 16)
            sp.dma_start(x0[:, :], x[:, 0:N]).then_inc(s["x_loaded"], 16)
            after(sp, "setup_dve", SETUP_DVE_STRIP)
            for m in range(2):
                for half in range(2):
                    first = strip[m * S:(m + 1) * S, :, :]
                    rows = bass.AP(tensor=first.tensor, offset=first.offset + (15 - half) * S,
                                   ap=[list(first.ap[0]), [-2 * S, 8], [1, 256]])
                    sp.dma_start(lines[:, m, half, :], rows).then_inc(s["lines_loaded"], 16)

            def step(k, first):
                l0, l3 = first < PAIRS, first >= 3
                value = (lambda v: v) if isinstance(k, int) else sp.snap
                now = value(k + 1)
                if l0 and first + 1 < PAIRS:
                    x_next = value((k + 1) * N)
                if l3:
                    done3, stored_at = value(k - 2), value((k - 3) * N)
                if l0:
                    after(sp, "gu_done", now)
                    after(sp, "toep_done", k)
                    sp.dma_start(seq[:, 1, :, :].rearrange("p a n -> p (a n)"),
                                 gu_col[S:2 * S, :].rearrange("s (b n) -> s b n", b=8)).then_inc(s["seq_loaded"], 16)
                    after(sp, "gu_row_done", now)
                    sp.dma_start(seq[:, 0, :, :].rearrange("p a n -> p (a n)"),
                                 gu_row[0:S, :].rearrange("s (b n) -> s b n", b=8)).then_inc(s["seq_loaded"], 16)
                    if first + 1 < PAIRS:
                        after(sp, "x0v0_done", now)
                        sp.dma_start(x0[:, :], x[:, bass.ds(x_next, N)]).then_inc(s["x_loaded"], 16)
                    after(sp, "d_done", k)
                    after(sp, "hs_read", now)
                    sp.dma_start(hs_row[C:C + S, :].rearrange("s (b n) -> s b n", b=8), hs[:, 0:2 * LN]
                                 ).then_inc(s["hs_loaded"], 16)
                    back = v_hs[C + S:128, :].rearrange("s (i b n) -> s i b n", i=NP, b=8)
                    for i in range(NP):
                        at = 2 * LN + i * 2 * W
                        sp.dma_start(back[:, i, :, :], hs[:, at:at + 2 * W]).then_inc(s["hs_loaded"], 16)
                if l3:
                    after(sp, "x_out_done", done3)
                    sp.dma_start(out[:, bass.ds(stored_at, N)], x_out[:, :]).then_inc(s["stored"], 16)

            for k in range(FILL):
                step(k, k)
            with sp.Fori(FILL, PAIRS - 1) as k:
                step(k, FILL)
            for k in range(PAIRS - 1, STEPS):
                step(k, k)
            sp.wait_ge(s["stored"], 16 * PAIRS)

        @block.tensor
        def _(pe):
            mm = nc.tensor.matmul
            pe.wait_ge(s["weights_in"], 16)
            mm(bank[0][0:32, 0:32], w("vt", 0, 16), w("ut", 0, 16), start=True, stop=True).then_inc(s["setup_pe"], 1)
            mm(bank[1][0:32, 0:32], w("ut", 0, 16), w("vt", 0, 16), start=True, stop=True).then_inc(s["setup_pe"], 1)
            for r, k in enumerate((1, 2, 4, 8)):
                n = min(k, 15 - k)
                after(pe, "setup_dve", SETUP_DVE_A + 2 * r)
                mm(bank[0][0:32, 0:n * 32], pw_b[:, k - 1, :], pw_a[:, 0:n, :], start=True, stop=True
                   ).then_inc(s["setup_pe"], 1)
                if k < 8:
                    mm(bank[1][0:32, 0:k * 32], pw_a[:, k - 1, :], pw_b[:, 0:k, :], start=True, stop=True
                       ).then_inc(s["setup_pe"], 1)
            after(pe, "setup_dve", SETUP_DVE_GN1)
            mm(bank[2][0:C, 0:GR], w("ones", 0, C), gn1[:, :], start=True, stop=True).then_inc(s["setup_pe"], 1)
            mm(bank[3][:, 0:GR], w("nb", 0, C).broadcast_to([C, 128]), w("g1", 0, C), start=True, stop=True).then_inc(s["setup_pe"], 1)
            mm(bank[4][:, 0:C], w("expand", 0, NF), w("filt", 0, NF), start=True, stop=True).then_inc(s["setup_pe"], 1)
            after(pe, "setup_dve", SETUP_DVE_ALL)
            after(pe, "setup_pool", 3)

            def step(k, first):
                l0, l1, l2a, l2b, l3 = active(first)
                gn = gn_range(first)
                if l2b:
                    j = k - 3
                    after(pe, "xw_done", j + 1)
                    for co in range(2):
                        for i, (n, ci) in enumerate([(n, ci) for n in range(NPT) for ci in range(2)]):
                            q = P8 * (1 + co - ci)
                            last = mm(p_conv[:, co * NP * C:(co + 1) * NP * C],
                                      bumps[:, n, q:q + P8, :].rearrange("p a b -> p (a b)"),
                                      xw[:, n, ci, :, :].rearrange("p a b -> p (a b)"),
                                      start=i == 0, stop=i == 2 * NPT - 1)
                    last.then_inc(s["conv2_done"], 1)
                if gn:
                    a, b = gn
                    after(pe, "gn3_moments", k - 3)
                    after(pe, "gn_e2", k + 1)
                    gn_product(a, b, "gn_group")
                if l2b:
                    after(pe, "spec_ready", k - 3)
                    after(pe, "y_pix_done", k - 2)
                    for i in range(NP):
                        for co in range(2):
                            at = i * PIX + co * HALF
                            last = nc.tensor.transpose(p_back[0:C, at:at + HALF], y_pix[:, co, i, :], w("ident"))
                    last.then_inc(s["back_done"], 1)
                if l3:
                    after(pe, "gn_moments", k + 1 if gn else PAIRS + 2)
                    after(pe, "gn3_e2", k - 2)
                    gn_product(3, 4, "gn3_group")
                if l0:
                    j = k
                    after(pe, "v_ready", k + 1)
                    after(pe, "d_read", j)
                    mm(p_proj[0:64, :], w("proj", 0, C), v0, start=True, stop=True).then_inc(s["proj_done"], 1)
                    after(pe, "hs_read", j)
                    for c in range(2 * NP):
                        mm(p_h[:, c, :], v0[:, c * HALF:(c + 1) * HALF], w("ln", 0, C), start=True, stop=True)
                    after(pe, "v0sq_done", j + 1)
                    for c in range(2 * NP):
                        last = mm(p_ssq[:, c:c + 1], v0sq[:, c * HALF:(c + 1) * HALF], w("ones", 0, C)[:, 0:1],
                                  start=True, stop=True)
                    last.then_inc(s["ssq_done"], 1)
                if l2a:
                    after(pe, "v_ready", k + 1)
                    if l2b:
                        after(pe, "y_pix_done", k - 2)
                    for ci in range(2):
                        for i in range(NP):
                            at = i * PIX + ci * HALF
                            o = (ci * NP + i) * C
                            last = nc.tensor.transpose(p_xt[:, o:o + C], v2[:, at:at + HALF], w("ident", 0, C)[:, 0:C])
                    last.then_inc(s["xt_done"], 1)
                if l3:
                    j = k - 3
                    after(pe, "v3_ready", j + 1)
                    after(pe, "tpad_done", j)
                    for c in range(2 * NP):
                        last = mm(p_t[:, c * C:(c + 1) * C], v3[:, c * HALF:(c + 1) * HALF], w("win3", 0, C),
                                  start=True, stop=True)
                    last.then_inc(s["t_done"], 1)
                if l1:
                    j = k - 1
                    after(pe, "v_ready", k + 1)
                    after(pe, "tanh_gate_done", j + 1)
                    mm(p_l1[0:C, :], w12[:, :], v1[:, :], start=True, stop=False)
                    after(pe, "max_done", j + 1)
                    mm(p_l1[0:C, :], w("w2", 0, C), max_all[:, :], start=False, stop=True).then_inc(s["l1_done"], 1)
                if l0:
                    j = k
                    if first == 0:
                        pe.wait_ge(s["toep_ready"], 1)
                    after(pe, "seq_loaded", 32 * (j + 1))
                    after(pe, "h_scaled_done", j + 1)
                    for m in range(2):
                        for mo in range(2):
                            for ci in range(2):
                                lhs = toep[:, m, ci, mo * 128:(mo + 1) * 128]
                                if m == 0:
                                    dst = p_toep[:, mo * LN:(mo + 1) * LN]
                                else:
                                    dst = p_toep[:, 2 * LN:4 * LN].rearrange("p (i a w) -> p a i w", i=NP, a=2)[:, mo]
                                last = mm(dst, lhs, seq[:, m, ci, :], start=ci == 0, stop=ci == 1)
                    last.then_inc(s["toep_done"], 1)
                if l3:
                    j = k - 3
                    after(pe, "t_pix_done", j + 1)
                    after(pe, "x3_done", j + 1)
                    mm(p_spec[:, 0:2 * NP * C], w("dft"), t_pix[:, :, :].rearrange("p a b -> p (a b)"),
                       start=True, stop=True).then_inc(s["spec_done"], 1)
                    after(pe, "spec_ready", j + 1)
                    for c in range(2 * NP):
                        last = mm(p_inv[0:CP, c * HALF:(c + 1) * HALF], spec[:, c, :], w("idft"), start=True, stop=True)
                    last.then_inc(s["inv_done"], 1)
                if l0:
                    j = k
                    after(pe, "h1_pix_done", j + 1)
                    if l1:
                        after(pe, "gelu1_done", k)
                    for c in range(2 * NP):
                        last = nc.tensor.transpose(p_h1[0:GR, c * HALF:(c + 1) * HALF], h1_pix[:, c, :], w("ident"))
                    last.then_inc(s["h1_back_done"], 1)
                    after(pe, "h1_done", j + 1)
                    mm(p_gate[0:C, :], w("g2", 0, GR), h1[:, :], start=True, stop=True).then_inc(s["gate_done"], 1)
                    after(pe, "hs_ready", j + 1)
                    after(pe, "hs_loaded", 48 * (j + 1))
                    after(pe, "proj_read", j + 1)
                    mm(p_d[0:C, :], dlhs, v_hs[:, :], start=True, stop=True).then_inc(s["d_done"], 1)
                if l3:
                    j = k - 3
                    after(pe, "prod3_done", j + 1)
                    after(pe, "x_out_done", j)
                    mm(p_out[0:C, :], w("wout3", MID, CP), prod3[MID:CP, :], start=True, stop=True
                       ).then_inc(s["out_done"], 1)

            def gn_product(a, b, event):
                n = (b - a) * NP * 2
                mm(p_gn[0:C, 0:n], w("group", 0, C),
                   stats[:, a:b, :, :].rearrange("p a i (f t) -> p (a i f) t", f=2)[:, :, 1], start=True, stop=True)
                mm(p_gn[0:C, n:2 * n], w("group", 0, C), halves[:, a:b, :, :].rearrange("p a i f -> p (a i f)"),
                   start=True, stop=True).then_inc(s[event], 1)

            for k in range(FILL):
                step(k, k)
            with pe.Fori(FILL, PAIRS) as k:
                step(k, FILL)
            for k in range(PAIRS, STEPS):
                step(k, k)

        @block.scalar
        def _(act):
            f = nc.scalar.activation
            act.wait_ge(s["weights_in"], 16)
            f(sig_a[:, 0:1], w("alog", 0, 32), ACT.Tanh, scale=0.5).then_inc(s["setup_act"], 1)
            after(act, "setup_dve", SETUP_DVE_ALL)
            after(act, "setup_pool", 3)

            def step(k, first):
                l0, l1, l2a, l2b, l3 = active(first)
                if l2b:
                    after(act, "conv2_done", k - 2)
                    f(y_pix[:, :, :, :].rearrange("p a b c -> p (a b c)"), p_conv[:, 0:2 * NP * C], ACT.Copy
                      ).then_inc(s["y_pix_done"], 1)
                if l0:
                    j = k
                    after(act, "v_ready", k + 1)
                    after(act, "ssq_done", j)
                    f(v0sq[:, :], v0, ACT.Square).then_inc(s["v0sq_done"], 1)
                    after(act, "proj_done", j + 1)
                    after(act, "gu_done", j)
                    hiw = "p (h i w) -> p i h w"
                    f(tanh_g[:, :].rearrange(hiw, i=NP, w=W), img(p_proj, 32, 64), ACT.Tanh, bias=w("bg", 0, 32),
                      scale=0.5)
                    f(u_half[:, :].rearrange(hiw, i=NP, w=W), img(p_proj, 0, 32), ACT.Identity, bias=w("bin", 0, 32)
                      ).then_inc(s["proj_read"], 1)
                    after(act, "ssq_done", j + 1)
                    after(act, "ln_var_done", j)
                    f(ln_msq[:, :], p_h[:, :, GR], ACT.Square).then_inc(s["ln_msq_done"], 1)
                if l3:
                    j = k - 3
                    after(act, "t_done", j + 1)
                    f(t_pix[:, :, :].rearrange("p a b -> p (a b)"), p_t[:, 0:2 * NP * C], ACT.Copy
                      ).then_inc(s["t_pix_done"], 1)
                if l0:
                    j = k
                    after(act, "gu_done", j + 1)
                    after(act, "seq_loaded", 32 * j)
                    f(gu_row[0:S, :].rearrange("p (w i h) -> p i h w", i=NP, h=H),
                      gu_col[0:S, :].rearrange("p (h i w) -> p i h w", i=NP, w=W), ACT.Copy
                      ).then_inc(s["gu_row_done"], 1)
                if l2a:
                    if l2b:
                        after(act, "x3_done", k - 2)
                    after(act, "x2_done", k - 1)
                    f(x2_late[:, :], x2[:, :], ACT.Copy).then_inc(s["x2_late_done"], 1)
                if l1:
                    j = k - 1
                    after(act, "l1_done", j + 1)
                    after(act, "x2_done", j)
                    f(gelu1[:, :], p_l1[0:C, :], ACT.Gelu, bias=bnb[:, :], scale=bns[:, :]).then_inc(s["gelu1_done"], 1)
                if l0:
                    j = k
                    after(act, "toep_done", j + 1)
                    after(act, "hs_loaded", 48 * j)
                    f(hs[:, :], p_toep[:, 0:4 * LN], ACT.Copy
                      ).then_inc(s["hs_read"], 1)
                    after(act, "h_in_done", j + 1)
                    after(act, "h1_back_done", j)
                    f(h1_pix[:, :, :], h_in[:, :, :], ACT.Gelu).then_inc(s["h1_pix_done"], 1)
                    after(act, "h1_back_done", j + 1)
                    after(act, "gate_done", j)
                    f(h1[:, :], p_h1[0:GR, :], ACT.Copy).then_inc(s["h1_done"], 1)
                if l3:
                    j = k - 3
                    after(act, "inv_done", j + 1)
                    after(act, "tap_done", 9 * j)
                    f(tpad[:, :, 1:1 + H, 1:1 + W], img(p_inv, 0, CP), ACT.Copy).then_inc(s["tpad_done"], 1)
                if l0:
                    j = k
                    after(act, "hs_loaded", 48 * (j + 1))
                    after(act, "d_done", j)
                    f(v_hs[C:C + S, :].rearrange("p (i h w) -> p i h w", i=NP, h=H),
                      hs_row[C:C + S, :].rearrange("p (w i h) -> p i h w", i=NP, h=H), ACT.Copy
                      ).then_inc(s["hs_ready"], 1)
                    after(act, "gate_done", j + 1)
                    after(act, "gated_done", j)
                    f(tanh_gate[:, :], p_gate[0:C, :], ACT.Tanh, bias=w("g2b", 0, C), scale=0.5
                      ).then_inc(s["tanh_gate_done"], 1)
                    after(act, "d_done", j + 1)
                    f(d_half[:, :], p_d[0:C, :], ACT.Identity, bias=dbias[:, :]).then_inc(s["d_read"], 1)
                if l3:
                    j = k - 3
                    after(act, "tap_done", 9 * (j + 1))
                    after(act, "prod3_done", j)
                    valid = conv[0:HID2, :, :]
                    g = img(gelu3, MID, CP)
                    for i in range(NP):
                        last = f(g[:, i, :, :], valid[:, i * HP:i * HP + H, :], ACT.Gelu)
                    last.then_inc(s["gelu3_done"], 1)

            for k in range(FILL):
                step(k, k)
            with act.Fori(FILL, PAIRS) as k:
                step(k, FILL)
            for k in range(PAIRS, STEPS):
                step(k, k)

        @block.gpsimd
        def _(pool):
            tt = nc.gpsimd.tensor_tensor
            nc.gpsimd.memset(tpad[:, :, :, :], 0.0)
            nc.gpsimd.memset(spec[:, :, HID2:MID], 0.0).then_inc(s["setup_pool"], 1)
            pool.wait_ge(s["weights_in"], 16)
            nc.gpsimd.tensor_scalar(bnv[:, :], w("var", 0, C), BN_EPS, None, ALU.add).then_inc(s["setup_pool"], 1)
            pool.wait_ge(s["setup_pool"], 2)
            tt(bnr[:, :], bnv[:, :], w("mhalf", 0, C)[:, 0:1], ALU.pow).then_inc(s["setup_pool"], 1)

            pool.wait_ge(s["lines_loaded"], 64)
            for m in range(2):
                for half in range(2):
                    last = nc.gpsimd.tensor_copy(toep[:, m, half, :].rearrange("p (a s b) -> p a s b", a=2, b=8),
                                                 lines[:, m, half, :].rearrange("p (b a s) -> p a s b", a=2, b=8))
            last.then_inc(s["toep_ready"], 1)

            def step(k, first):
                l0, l1, l2a, l2b, l3 = active(first)
                gn = gn_range(first)
                if gn:
                    a, b = gn
                    after(pool, "gn_var", k + 1)
                    after(pool, "v_ready", k)
                    tt(rstd[:, a:b, :], gvar[:, a:b, :],
                       w("mhalf", 0, C)[:, 0:(b - a) * NP].rearrange("p (a b) -> p a b", b=NP), ALU.pow
                       ).then_inc(s["gn_rstd"], 1)
                if l3:
                    after(pool, "gn3_var", k - 2)
                    after(pool, "v3_ready", k - 3)
                    tt(rstd[:, 3, :], gvar[:, 3, :], w("mhalf", 0, C)[:, 0:NP], ALU.pow).then_inc(s["gn3_rstd"], 1)
                if l0:
                    j = k
                    after(pool, "v_ready", k + 1)
                    after(pool, "x1_done", j)
                    tt(x0v0[:, :], x0[:, :], v0, ALU.add).then_inc(s["x0v0_done"], 1)
                if l0:
                    j = k
                    after(pool, "ln_var_done", j + 1)
                    after(pool, "h_scaled_done", j)
                    tt(ln_rstd[:, :], ln_var[:, :], w("mhalf")[:, 0:2 * NP], ALU.pow
                       ).then_inc(s["ln_rstd_done"], 1)
                if l1:
                    j = k - 1
                    after(pool, "gelu1_done", j + 1)
                    after(pool, "x1_done", j + 1)
                    if l2a:
                        after(pool, "v_ready", k + 1)
                        after(pool, "x2_late_done", k - 1)
                    tt(x2[:, :], x1[:, :], gelu1[:, :], ALU.add).then_inc(s["x2_done"], 1)
                if l0:
                    j = k
                    after(pool, "gated_done", j + 1)
                    after(pool, "x0v0_done", j + 1)
                    if l1:
                        after(pool, "v_ready", k + 1)
                        after(pool, "x2_done", k)
                    tt(x1[:, :], x0v0[:, :], gated[:, :], ALU.add).then_inc(s["x1_done"], 1)

            for k in range(FILL):
                step(k, k)
            with pool.Fori(FILL, PAIRS) as k:
                step(k, FILL)
            for k in range(PAIRS, STEPS):
                step(k, k)

        @block.vector
        def _(dve):
            tt, ts, stt = nc.vector.tensor_tensor, nc.vector.tensor_scalar, nc.vector.scalar_tensor_tensor
            copy = nc.vector.tensor_copy
            count = [0]

            def link(ins):
                count[0] += 1
                ins.then_inc(s["setup_dve"], 1)
                dve.wait_ge(s["setup_dve"], count[0])

            dve.wait_ge(s["weights_in"], 16)
            dve.wait_ge(s["setup_act"], 1)
            link(ts(sig_a[:, 1:2], sig_a[:, 0:1], 0.5, 0.5, ALU.mult, ALU.add))
            dve.wait_ge(s["setup_pe"], 2)
            link(stt(pw_a[:, 0, :], w("id32", 0, 32), sig_a[:, 1:2], bank[0][0:32, 0:32], ALU.mult, ALU.add))
            link(stt(pw_b[:, 0, :], w("id32", 0, 32), sig_a[:, 1:2], bank[1][0:32, 0:32], ALU.mult, ALU.add))
            assert count[0] == SETUP_DVE_A
            got = 2
            for k in (1, 2, 4, 8):
                n = min(k, 15 - k)
                got += 2 if k < 8 else 1
                dve.wait_ge(s["setup_pe"], got)
                link(copy(pw_a[:, k:k + n, :].rearrange("p a b -> p (a b)"), bank[0][0:32, 0:n * 32]))
                if k < 8:
                    n = min(k, 8 - k)
                    link(copy(pw_b[:, k:k + n, :].rearrange("p a b -> p (a b)"), bank[1][0:32, 0:n * 32]))
            link(tt(strip[:, 16:31, :], pw_a[:, :, 0:S], pw_a[:, :, S:2 * S], ALU.add))
            link(tt(strip[:, 14::-1, :], pw_a[:, :, 0:S], pw_a[:, :, S:2 * S], ALU.add))
            link(tt(strip[:, 15, :], w("id32", 0, 32)[:, 0:S], w("id32", 0, 32)[:, S:2 * S], ALU.add))
            link(ts(strip[:, 15, :], strip[:, 15, :], 2.0, None, ALU.mult))
            assert count[0] == SETUP_DVE_STRIP, count[0]
            link(ts(gn1[:, :], w("g1", 0, C), w("nw", 0, C), None, ALU.mult))
            assert count[0] == SETUP_DVE_GN1, count[0]
            at = cols["proj"][0]
            link(ts(wt[0:C, at:at + 32], wt[0:C, at:at + 32], 0.5, None, ALU.mult))
            dve.wait_ge(s["setup_pe"], got + 1)
            link(tt(w("ln", 0, C)[:, 0:GR], gn1[:, :], bank[2][0:C, 0:GR], ALU.subtract))
            dve.wait_ge(s["setup_pe"], got + 2)
            link(tt(hbias[:, :], w("g1b"), bank[3][:, 0:GR], ALU.add))
            dve.wait_ge(s["setup_pe"], got + 3)
            link(copy(filt[:, :], bank[4][:, 0:C]))
            link(ts(w("bin", 0, 32), w("bin", 0, 32), 0.5, None, ALU.mult))
            link(ts(w("bg", 0, 32), w("bg", 0, 32), 0.5, None, ALU.mult))
            link(ts(w("g2b", 0, C), w("g2b", 0, C), 0.5, None, ALU.mult))
            link(tt(dsum[:, :], w("skr", 0, C), w("skc", 0, C), ALU.add))
            link(stt(dlhs[0:C, :], dsum[:, :], 0.25, w("halfid", 0, C), ALU.mult, ALU.subtract))
            link(ts(dlhs[C:128, :], dlhs[C:128, :], 0.125, None, ALU.mult))
            link(nc.vector.tensor_reduce(dbias[:, :], w("dbias", 0, C), AX.X, ALU.add))
            link(ts(dbias[:, :], dbias[:, :], 0.25, None, ALU.mult))
            link(tt(w12[:, :], w("w1", 0, C), w("w2", 0, C), ALU.subtract))
            dve.wait_ge(s["setup_pool"], 3)
            link(tt(bns[:, :], bnr[:, :], w("gamma", 0, C), ALU.mult))
            link(tt(bnd[:, :], w("cb", 0, C), w("mean", 0, C), ALU.subtract))
            link(stt(bnb[:, :], bnd[:, :], bns[:, :], w("beta", 0, C), ALU.mult, ALU.add))
            link(nc.vector.reciprocal(rinv[:, :], w("rad")))
            link(ts(nrinv[:, :], rinv[:, :], -1.0, None, ALU.mult))
            wc = w("wc")
            for n in range(NPT):
                ts(axd[:, n, :], w("dx"), wc[:, 2 * n:2 * n + 1], None, ALU.subtract)
                last = ts(ayd[:, n, :], w("dy"), wc[:, 2 * n + 1:2 * n + 2], None, ALU.add)
            link(last)
            stt(axa[:, :, :], axd[:, :, :], -1.0, axd[:, :, :], ALU.mult, ALU.max)
            link(stt(aya[:, :, :], ayd[:, :, :], -1.0, ayd[:, :, :], ALU.mult, ALU.max))
            for n in range(NPT):
                stt(ax[:, n, :], axa[:, n, :], rinv[:, n:n + 1], w("bigx"), ALU.mult, ALU.add)
                last = stt(ay[:, n, :], aya[:, n, :], nrinv[:, n:n + 1], w("oney"), ALU.mult, ALU.add)
            link(last)
            for n in range(NPT):
                last = tt(graw[:, n, :, :], ay[:, n, :].unsqueeze(2).broadcast_to([128, WIN, W]),
                          ax[:, n, :].unsqueeze(1).broadcast_to([128, WIN, W]), ALU.subtract)
            link(last)
            link(ts(bumps[:, :, :, :].rearrange("p a b c -> p (a b c)"),
                    graw[:, :, :, :].rearrange("p a b c -> p (a b c)"), 0.0, None, ALU.max))
            assert count[0] == SETUP_DVE_ALL, count[0]
            dve.wait_ge(s["setup_pool"], 3)

            def statistics(a, b, ready, events, n):
                for st in range(a, b):
                    ready(st)
                    for i in range(NP):
                        last = nc.vector.bn_stats(stats[:, st, i, :], xs[st][:, i * PIX:(i + 1) * PIX])
                last.then_inc(s[events[0]], 1)
                dve.wait_ge(s[events[0]], n)
                t = stats[:, a:b, :, :].rearrange("p a i (f t) -> p (a i f) t", f=2)
                q = "p a i f -> p (a i f)"
                tt(squares[:, a:b, :, :].rearrange(q), t[:, :, 1], t[:, :, 1], ALU.mult).then_inc(s[events[1]], 1)
                dve.wait_ge(s[events[1]], n)
                stt(halves[:, a:b, :, :].rearrange(q), t[:, :, 2], 2.0 / PIX, squares[:, a:b, :, :].rearrange(q),
                    ALU.mult, ALU.add).then_inc(s[events[2]], 1)

            def group_variance(a, b, events, n):
                m = (b - a) * NP
                dve.wait_ge(s[events[0]], n)
                nc.vector.tensor_reduce(moments[:, :, a:b, :], p_gn[0:C, 0:4 * m].rearrange(
                    "p (q a i f) -> p q a i f", q=2, a=b - a, i=NP), AX.X, ALU.add).then_inc(s[events[1]], 1)
                dve.wait_ge(s[events[1]], n)
                tt(msq[:, a:b, :], moments[:, 0, a:b, :], moments[:, 0, a:b, :], ALU.mult).then_inc(s[events[2]], 1)
                dve.wait_ge(s[events[2]], n)
                q = "p a i -> p (a i)"
                stt(gvar[:, a:b, :].rearrange(q), moments[:, 1, a:b, :].rearrange(q), GN_EPS,
                    msq[:, a:b, :].rearrange(q), ALU.add, ALU.subtract).then_inc(s[events[3]], 1)

            def normalise(st):
                for i in range(NP):
                    at = slice(i * PIX, (i + 1) * PIX)
                    last = ts(vs[st][:, at], xs[st][:, at], moments[:, 0, st, i:i + 1], rstd[:, st, i:i + 1],
                              ALU.subtract, ALU.mult)
                return last

            def step(k, first):
                l0, l1, l2a, l2b, l3 = active(first)
                gn = gn_range(first)
                if gn:
                    def ready(st):
                        if st == 0:
                            dve.wait_ge(s["x_loaded"], 16 * (k + 1))
                        elif st == 1:
                            dve.wait_ge(s["x1_done"], k)
                        else:
                            dve.wait_ge(s["x2_done"], k - 1)
                    statistics(*gn, ready, ("gn_stats", "gn_sq", "gn_e2"), k + 1)
                if l2b:
                    j = k - 3
                    after(dve, "back_done", j + 1)
                    after(dve, "x2_late_done", j + 1)
                    after(dve, "x_out_done", j)
                    tt(x3[:, :], x2_late[:, :], p_back[0:C, :], ALU.add).then_inc(s["x3_done"], 1)
                    statistics(3, 4, lambda st: dve.wait_ge(s["x3_done"], j + 1),
                               ("gn3_stats", "gn3_sq", "gn3_e2"), j + 1)
                if gn:
                    group_variance(*gn, ("gn_group", "gn_moments", "gn_msq", "gn_var"), k + 1)
                if l3:
                    group_variance(3, 4, ("gn3_group", "gn3_moments", "gn3_msq", "gn3_var"), k - 2)
                if gn:
                    after(dve, "gn_rstd", k + 1)
                    if l0:
                        after(dve, "d_done", k)
                        after(dve, "x0v0_done", k)
                        after(dve, "v0sq_done", k)
                    if l1:
                        after(dve, "l1_done", k - 1)
                        after(dve, "horiz_done", k - 1)
                    if l2a:
                        after(dve, "xt_done", k - 2)
                    for st in range(*gn):
                        last = normalise(st)
                    last.then_inc(s["v_ready"], 1)
                if l3:
                    j = k - 3
                    after(dve, "gn3_rstd", j + 1)
                    after(dve, "t_done", j)
                    normalise(3).then_inc(s["v3_ready"], 1)
                if l0:
                    j = k
                    after(dve, "proj_read", j + 1)
                    after(dve, "gu_row_done", j)
                    after(dve, "seq_loaded", 32 * j)
                    stt(gu_col[:, :], tanh_g[:, :], 1.0, u_half[:, :], ALU.add, ALU.mult).then_inc(s["gu_done"], 1)
                if l1:
                    j = k - 1
                    v, m1, m2, m = img(v1), img(max_v1), img(max_v2), img(max_h)
                    after(dve, "v_ready", k + 1)
                    after(dve, "max_done", j)
                    tt(m1[:, :, 0:H - 2, :], v[:, :, 0:H - 2, :], v[:, :, 2:H, :], ALU.max)
                    tt(m1[:, :, H - 2:H, :], v[:, :, H - 2:H, :], v[:, :, 0:2, :], ALU.max).then_inc(s["vert1_done"], 1)
                    after(dve, "vert1_done", j + 1)
                    tt(m2[:, :, 2:H, :], m1[:, :, 2:H, :], m1[:, :, 0:H - 2, :], ALU.max)
                    tt(m2[:, :, 0:2, :], m1[:, :, 0:2, :], m1[:, :, H - 2:H, :], ALU.max).then_inc(s["vert2_done"], 1)
                    tt(m[:, :, :, 2:W - 2], v[:, :, :, 0:W - 4], v[:, :, :, 4:W], ALU.max)
                    tt(m[:, :, :, 0:2], v[:, :, :, W - 2:W], v[:, :, :, 2:4], ALU.max)
                    tt(m[:, :, :, W - 2:W], v[:, :, :, W - 4:W - 2], v[:, :, :, 0:2], ALU.max
                       ).then_inc(s["horiz_done"], 1)
                if l2a:
                    j = k - 2
                    after(dve, "xt_done", j + 1)
                    after(dve, "conv2_done", j)
                    for n in range(NPT):
                        last = tt(xw[:, n, :, :, :].rearrange("p a b c -> p (a b) c"),
                                  p_xt[:, 0:2 * NP * C].rearrange("p (a c) -> p a c", c=C),
                                  w("wb")[:, n * C:(n + 1) * C].unsqueeze(1).broadcast_to([128, 2 * NP, C]), ALU.mult)
                    last.then_inc(s["xw_done"], 1)
                if l0:
                    j = k
                    after(dve, "ssq_done", j + 1)
                    after(dve, "ln_msq_done", j + 1)
                    after(dve, "ln_rstd_done", j)
                    stt(ln_var[:, :], p_ssq, LN_EPS, ln_msq[:, :], ALU.add, ALU.subtract
                        ).then_inc(s["ln_var_done"], 1)
                if l1:
                    j = k - 1
                    after(dve, "vert2_done", j + 1)
                    after(dve, "horiz_done", j + 1)
                    after(dve, "l1_done", j)
                    tt(max_all[:, :], max_v2[:, :], max_h[:, :], ALU.max).then_inc(s["max_done"], 1)
                if l0:
                    j = k
                    after(dve, "ln_rstd_done", j + 1)
                    after(dve, "h1_pix_done", j)
                    tt(h_scaled[:, :, :], p_h[:, :, 0:GR], ln_rstd[:, :].unsqueeze(2).broadcast_to([128, 2 * NP, GR]),
                       ALU.mult).then_inc(s["h_scaled_done"], 1)
                    after(dve, "h_scaled_done", j + 1)
                    tt(h_in[:, :, :], h_scaled[:, :, :], hbias[:, :].unsqueeze(1).broadcast_to([128, 2 * NP, GR]),
                       ALU.add).then_inc(s["h_in_done"], 1)
                if l3:
                    j = k - 3
                    after(dve, "spec_done", j + 1)
                    after(dve, "inv_done", j)
                    halves_of = "p a (b c) -> p a b c"
                    z = bass.AP(tensor=spec[:, :, :].tensor, offset=spec[:, :, :].offset,
                                ap=[list(spec[:, :, :].ap[0]), [CP, 2 * NP], [MID, 2], [1, HID2]])
                    tt(z, p_spec[:, 0:2 * NP * C].rearrange("p (a b c) -> p a b c", b=2, c=HID2),
                       filt[:, :].rearrange("p (b c) -> p b c", b=2).unsqueeze(1).broadcast_to([128, 2 * NP, 2, HID2]),
                       ALU.mult).then_inc(s["spec_ready"], 1)
                if l3:
                    j = k - 3
                    after(dve, "tpad_done", j + 1)
                    after(dve, "gelu3_done", j)
                    after(dve, "prod3_done", j)
                    rows = tpad[:, :, :, :].rearrange("p i h w -> p (i h) w")
                    taps = w("wdw", 0, CP)
                    for t in range(9):
                        src = rows[:, t // 3:t // 3 + ROWS, t % 3:t % 3 + W]
                        if t == 0:
                            ts(conv[:, :, :], src, taps[:, t:t + 1], None, ALU.mult).then_inc(s["tap_done"], 1)
                        else:
                            after(dve, "tap_done", 9 * j + t)
                            stt(conv[:, :, :], src, taps[:, t:t + 1], conv[:, :, :], ALU.mult, ALU.add
                                ).then_inc(s["tap_done"], 1)
                if l0:
                    j = k
                    after(dve, "tanh_gate_done", j + 1)
                    after(dve, "d_read", j + 1)
                    after(dve, "x1_done", j)
                    stt(gated[:, :], tanh_gate[:, :], 1.0, d_half[:, :], ALU.add, ALU.mult).then_inc(s["gated_done"], 1)
                if l3:
                    j = k - 3
                    after(dve, "gelu3_done", j + 1)
                    after(dve, "tap_done", 9 * (j + 1))
                    after(dve, "out_done", j)
                    g, p = img(gelu3, MID, CP), img(prod3, MID, CP)
                    for i in range(NP):
                        last = tt(p[:, i, :, :], g[:, i, :, :], conv[MID:CP, i * HP:i * HP + H, :], ALU.mult)
                    last.then_inc(s["prod3_done"], 1)
                    after(dve, "out_done", j + 1)
                    after(dve, "stored", 16 * j)
                    tt(x_out[:, :], x3[:, :], p_out[0:C, :], ALU.add).then_inc(s["x_out_done"], 1)

            for k in range(FILL):
                step(k, k)
            with dve.Fori(FILL, PAIRS) as k:
                step(k, FILL)
            for k in range(PAIRS, STEPS):
                step(k, k)


def packed_weights(a):
    cols, n = weight_layout()
    wt = np.zeros((128, n), np.float32)

    def put(name, value, p0=0, c0=0):
        value = np.asarray(value)
        if value.ndim == 1:
            value = value[:, None]
        at = cols[name][0] + c0
        wt[p0:p0 + value.shape[0], at:at + value.shape[1]] = value

    for name, value in shape_constants().items():
        put(name, value)
    put("ln", np.full((C, 1), 1.0 / C), c0=GR)
    for i, d in enumerate(("row", "col")):
        g = {key: a[f"L0_conv_{d}_{key}"] for key in ("a_logit", "U", "V", "Win", "bin", "Wg", "bg", "Wout", "bout",
                                                      "Wskip", "bskip")}
        put("proj", g["Win"].T, c0=i * S)
        put("proj", g["Wg"].T, c0=32 + i * S)
        put("bin", g["bin"], p0=i * S)
        put("bg", g["bg"], p0=i * S)
        put("alog", g["a_logit"], p0=i * S)
        put("vt", g["V"].T, p0=i * R, c0=i * S)
        put("ut", g["U"].T, p0=i * R, c0=i * S)
        put("skr" if i == 0 else "skc", g["Wskip"].T)
        put("dlhs", g["Wout"].T, p0=C + i * S)
        put("dbias", g["bout"], c0=2 * i)
        put("dbias", g["bskip"], c0=2 * i + 1)
    put("g1", a["L0_conv_g1_w"].T)
    put("g1b", np.broadcast_to(a["L0_conv_g1_b"].reshape(1, GR), (128, GR)))
    put("nw", a["L0_conv_norm_w"])
    put("nb", a["L0_conv_norm_b"])
    put("g2", a["L0_conv_g2_w"].T)
    put("g2b", a["L0_conv_g2_b"])
    put("w1", a["L1_conv_conv_w"][:, :C].T)
    put("w2", a["L1_conv_conv_w"][:, C:].T)
    for name, key in (("cb", "conv_b"), ("gamma", "bn_gamma"), ("beta", "bn_beta"), ("mean", "bn_mean"),
                      ("var", "bn_var")):
        put(name, a["L1_conv_" + key])
    put("wc", np.broadcast_to(a["L2_conv_weight_coord"].reshape(1, 2 * NPT), (128, 2 * NPT)))
    put("rad", np.broadcast_to(a["L2_conv_radius"].reshape(1, NPT), (128, NPT)))
    put("wb", np.broadcast_to(a["L2_conv_weights"][0].T.reshape(1, NPT * C), (128, NPT * C)))
    put("filt", a["L3_conv_fft_filter"].reshape(C, NF).T)
    put("win3", a["L3_conv_w_in"].T)
    put("wout3", a["L3_conv_w_out"].T, p0=MID)
    taps = a["L3_conv_w_dw"].reshape(C, 9)
    put("wdw", taps[:HID2])
    put("wdw", taps[HID2:], p0=MID)
    return wt


def kernel(**inputs):
    import concourse.bacc as bacc
    from concourse.bass_utils import run_bass_kernel_spmd

    a = {name: np.asarray(value) for name, value in inputs.items()}
    nc = bacc.Bacc("TRN2", target_bir_lowering=False, num_devices=1)
    arrays = {
        "x_channels": np.ascontiguousarray(a["x"].transpose(1, 0, 2, 3).reshape(C, B * PIX)),
        "weights_packed": packed_weights(a),
    }
    args = [nc.dram_tensor(name, v.shape, mybir.dt.from_np(v.dtype), kind="ExternalInput").ap()
            for name, v in arrays.items()]
    out = nc.dram_tensor("out_channels", (C, B * PIX), mybir.dt.float32, kind="ExternalOutput").ap()
    build(nc, *args, out)
    got = run_bass_kernel_spmd(nc, [arrays], core_ids=[0]).results[0]["out_channels"]
    return np.ascontiguousarray(got.reshape(C, B, H, W).transpose(1, 0, 2, 3))
```

```python
import numpy as np
import concourse.bass as bass
from concourse import mybir
from contextlib import ExitStack

B, C, H, W = 16, 96, 16, 16
S, R, GR = 16, 8, 16
NP = 2
PAIRS = B // NP
PIX = H * W
N = NP * PIX
HALF = PIX // 2
LN = H * NP
K2, PAD2, NPT = 11, 5, 4
P8 = 8
NF = P8 * (P8 // 2 + 1)
HID2 = C // 2
MID = 64
CP = MID + HID2
WP = W + 2
HP = H + 1
ROWS = NP * HP - 1
WIN = 3 * P8
BIG = 1e30
GN_EPS, LN_EPS, BN_EPS = 1e-5, 1e-6, 1e-5


STEPS = PAIRS + 5
XW_DVE, XW_POOL = (0, 1), (2, 3)
FILL = 6


def active(step):
    return tuple(age <= step < PAIRS + age for age in range(6))


def gn_range(step):
    on = [b for b, age in ((1, 1), (2, 2), (3, 4)) if age <= step < PAIRS + age]
    return (on[0], on[-1] + 1) if on else None


def weight_layout():
    cols, at = {}, 0
    for name, n in [("proj", 64), ("ln", GR + 1), ("group", C), ("ones", C), ("g1", GR), ("nw", 1), ("nb", 1), ("g1b", GR),
                    ("bin", 1), ("bg", 1), ("alog", 1), ("vt", 32), ("ut", 32), ("id32", 32), ("g2", C), ("g2b", 1),
                    ("skr", C), ("skc", C), ("halfid", C), ("dlhs", C), ("dbias", 4),
                    ("w1", C), ("w2", C), ("cb", 1), ("gamma", 1), ("beta", 1), ("mean", 1), ("var", 1),
                    ("wc", 2 * NPT), ("rad", NPT), ("dx", W), ("bigx", W), ("dy", WIN), ("oney", WIN), ("wb", NPT * C),
                    ("win3", C), ("wout3", C), ("wdw", 9), ("filt", C), ("expand", 128), ("dft", 128), ("idft", 128),
                    ("ident", 128), ("mhalf", 16), ("mone", 16)]:
        cols[name] = (at, n)
        at += n
    return cols, at


def shape_constants():
    c = {}
    c["group"] = np.kron(np.eye(32), np.ones((3, 3))) / 6.0
    c["ones"] = np.full((C, C), 1.0 / C)
    c["halfid"] = 0.5 * np.eye(C)
    c["id32"] = np.eye(32)
    c["ident"] = np.eye(128)
    c["mhalf"] = np.full((128, 16), -0.5)
    c["mone"] = np.full((128, 16), -1.0)
    yl, xi = np.divmod(np.arange(128), W)
    xo, q = np.arange(W), np.arange(-P8, 2 * P8)
    dx, dy = xi[:, None] - xo[None], yl[:, None] - q[None]
    c["dx"], c["dy"] = dx / PAD2, dy / PAD2
    c["bigx"] = np.where(np.abs(dx) <= PAD2, 0.0, BIG)
    c["oney"] = np.where(np.abs(dy) <= PAD2, 1.0, 1.0 - BIG)
    y, x = np.mgrid[0:P8, 0:P8]
    basis, expand = [], []
    for kx in range(P8 // 2 + 1):
        for ky in range(P8):
            own = np.zeros(NF)
            if kx in (0, P8 // 2):
                if ky > P8 // 2:
                    continue
                own[ky * 5 + kx] += 0.5
                own[(P8 - ky) % P8 * 5 + kx] += 0.5
            else:
                own[ky * 5 + kx] = 1.0
            angle = 2 * np.pi * (ky * y + kx * x) / P8
            if kx in (0, P8 // 2) and ky in (0, P8 // 2):
                basis.append(np.cos(angle) / P8)
                expand.append(own)
            else:
                basis += [np.sqrt(2) / P8 * np.cos(angle), np.sqrt(2) / P8 * np.sin(angle)]
                expand += [own, own]
    basis = np.array(basis)
    dft = np.zeros((P8, 2, P8, 2, 64))
    for b in range(2):
        dft[:, b, :, b, :] = basis.transpose(1, 2, 0)
    c["dft"] = dft.reshape(128, 128)
    c["idft"] = c["dft"].T
    c["expand"] = np.tile(np.array(expand).T, (1, 2))
    return c


def build(nc, x, wts, out):
    F32 = mybir.dt.float32
    ALU = mybir.AluOpType
    ACT = mybir.ActivationFunctionType
    AX = mybir.AxisListType
    cols, NW = weight_layout()

    ctx = ExitStack()
    with ctx:
        def sb(name, shape):
            return ctx.enter_context(nc.sbuf_tensor(name, shape, F32))

        def sem(name):
            return ctx.enter_context(nc.semaphore(name))

        wt = sb("weights", [128, NW])

        def w(name, p0=0, p1=128):
            at, n = cols[name]
            return wt[p0:p1, at:at + n]

        x0, x1, x2, x3 = (sb(f"x{i}", [C, N]) for i in range(4))
        x2_late, x3_late = sb("x2_late", [C, N]), sb("x3_late", [C, N])
        x_out, x0v0 = sb("x_out", [C, N]), sb("x0v0", [C, N])
        v_hs = sb("v_hs", [128, N])
        v0 = v_hs[0:C, :]
        v1, v2, v3 = (sb(f"v{i}", [C, N]) for i in range(1, 4))
        xs, vs = [x0, x1, x2, x3], [v0, v1, v2, v3]
        stats = sb("stats", [C, 4, NP, 6])
        halves = sb("halves", [C, 4, NP, 2])
        squares = sb("squares", [C, 4, NP, 2])
        moments = sb("moments", [C, 2, 4, NP])
        msq = sb("msq", [C, 4, NP])
        gvar = sb("gvar", [C, 4, NP])
        rstd = sb("rstd", [C, 4, NP])
        neg_mean, shift = sb("neg_mean", [C, 4, NP]), sb("shift", [C, 4, NP])
        v0sq = sb("v0sq", [C, N])
        tanh_g, u_half = sb("tanh_g", [32, N]), sb("u_half", [32, N])
        ln_msq, ln_var, ln_rstd = (sb(n, [128, 2 * NP]) for n in ("ln_msq", "ln_var", "ln_rstd"))
        gu_col = sb("gu_col", [32, N])
        gu_row = sb("gu_row", [32, N])
        seq = sb("seq", [128, 2, 2, LN])
        hs = sb("hs", [128, 4 * LN])
        hs_row = sb("hs_row", [128, N])
        h_scaled, h_in, h1_pix = (sb(n, [128, 2 * NP, GR]) for n in ("h_scaled", "h_in", "h1_pix"))
        h1 = sb("h1", [GR, N])
        tanh_gate, d_half, gated = sb("tanh_gate", [C, N]), sb("d_half", [C, N]), sb("gated", [C, N])
        max_v1, max_v2, max_h, max_all = (sb(f"max{i}", [C, N]) for i in range(4))
        gelu1 = sb("gelu1", [C, N])
        bumps = sb("bumps", [128, NPT, WIN, W])
        x_pix = sb("x_pix", [128, 2 * NP, C])
        xw = sb("xw", [128, NPT, 2, NP, C])
        y_pix = sb("y_pix", [128, 2, NP, C])
        t_pix = sb("t_pix", [128, 2 * NP, C])
        filt = sb("filt_spec", [128, C])
        spec = sb("spec", [128, 2 * NP, CP])
        tpad = sb("tpad", [CP, NP * HP + 1, WP])
        tap_a, tap_b, two_taps = (sb(n, [CP, ROWS, W]) for n in ("tap_a", "tap_b", "two_taps"))
        conv = sb("conv", [CP, ROWS, W])
        gelu3, prod3 = sb("gelu3", [CP, N]), sb("prod3", [CP, N])
        gn1, hbias = sb("gn1", [C, GR]), sb("hbias", [128, GR])
        dlhs = w("dlhs")
        dsum, dbias = sb("dsum", [C, C]), sb("dbias_half", [C, 1])
        w12, bnv, bnr, bns, bnd, bnb = sb("w12", [C, C]), *(sb(f"bn{i}", [C, 1]) for i in range(5))
        sig_a = sb("sig_a", [32, 2])
        pw_a, pw_b = sb("pw_a", [32, 15, 32]), sb("pw_b", [32, 8, 32])
        strip = sb("strip", [32, 31, S])
        lines = sb("lines", [128, 2, 2, 256])
        toep = sb("toep", [128, 2, 2, 256])
        rinv, nrinv = sb("rinv", [128, NPT]), sb("nrinv", [128, NPT])
        axd, ax = sb("axd", [128, NPT, W]), sb("ax", [128, NPT, W])
        ayd, ay = sb("ayd", [128, NPT, WIN]), sb("ay", [128, NPT, WIN])
        axa, aya = sb("axa", [128, NPT, W]), sb("aya", [128, NPT, WIN])
        graw = sb("graw", [128, NPT, WIN, W])

        bank = [ctx.enter_context(nc.psum_tensor(f"bank{i}", [128, 512], F32)) for i in range(8)]
        p_gn, p_spec = bank[0], bank[0]
        p_proj, p_d = bank[1], bank[1]
        p_ln, p_toep = bank[2], bank[2]
        p_h, p_ssq = p_ln[:, 0:2 * NP * (GR + 1)].rearrange("p (a b) -> p a b", a=2 * NP), p_ln[:, 128:128 + 2 * NP]
        p_l1, p_h1, p_gate = bank[3], bank[3], bank[3]
        p_conv, p_xt = bank[4], bank[4]
        p_back = bank[5]
        p_t, p_inv = bank[6], bank[6]
        p_out = bank[7]

        names = """weights_in x_loaded gn0_stats gn0_sq gn0_e2 gn0_group gn0_moments gn0_msq gn0_var gn0_neg gn0_rstd
        gn0_shift gn_stats gn_sq gn_e2 gn_group gn_moments gn_msq gn_var gn_neg gn_rstd gn_shift
        v0_ready v1_ready v2_ready v3_ready
        proj_done v0sq_done ssq_done proj_read gu_done gu_row_done seq_loaded toep_done hs_read hs_loaded hs_ready
        ln_msq_done ln_var_done ln_rstd_done h_scaled_done h_in_done h1_pix_done h1_back_done h1_done gate_done
        tanh_gate_done d_done d_read gated_done x0v0_done x1_done
        vert1_done vert2_done horiz_done max_done l1_done gelu1_done x2_done x2_late_done
        xt_done x_pix_done xw_done xw_pool_done conv2_done y_pix_done back_done x3_done x3_late_done
        t_done t_pix_done spec_done spec_ready inv_done tpad_done taps_ab_done two_taps_done tap_done
        gelu3_done prod3_done out_done x_out_done stored
        setup_pe setup_dve setup_act setup_pool powers_done strip_done gn1_done setup_steps lines_loaded toep_ready""".split()
        s = {n: sem(n) for n in names}
        per_pair = {"x_loaded": 16, "seq_loaded": 32, "hs_loaded": 48, "tap_done": 7, "stored": 16}

        def after(eng, name, count):
            if isinstance(count, int):
                if not name.startswith(("gn_", "setup", "powers")):
                    count = min(count, PAIRS * per_pair.get(name, 1))
                if count <= 0:
                    return
            eng.wait_ge(s[name], count)

        def img(t, p0=0, p1=None):
            return t[p0:p1, :].rearrange("p (i h w) -> p i h w", i=NP, h=H)

        block = ctx.enter_context(nc.Block())

        @block.sync
        def _(sp):
            sp.dma_start(wt[:, :], wts).then_inc(s["weights_in"], 16)
            sp.dma_start(x0[:, :], x[:, 0:N]).then_inc(s["x_loaded"], 16)
            after(sp, "strip_done", 1)
            for m in range(2):
                for half in range(2):
                    first = strip[m * S:(m + 1) * S, :, :]
                    rows = bass.AP(tensor=first.tensor, offset=first.offset + (15 - half) * S,
                                   ap=[list(first.ap[0]), [-2 * S, 8], [1, 256]])
                    sp.dma_start(lines[:, m, half, :], rows).then_inc(s["lines_loaded"], 16)

            def step(k, first):
                l0, l3b = first < PAIRS, first >= 5
                value = (lambda v: v) if isinstance(k, int) else sp.snap
                now = value(k + 1)
                if l0 and first + 1 < PAIRS:
                    x_next = value((k + 1) * N)
                if l3b:
                    done3, stored_at = value(k - 4), value((k - 5) * N)
                if l0:
                    after(sp, "gu_done", now)
                    after(sp, "toep_done", k)
                    sp.dma_start(seq[:, 1, :, :].rearrange("p a n -> p (a n)"),
                                 gu_col[S:2 * S, :].rearrange("s (b n) -> s b n", b=8)).then_inc(s["seq_loaded"], 16)
                    after(sp, "gu_row_done", now)
                    sp.dma_start(seq[:, 0, :, :].rearrange("p a n -> p (a n)"),
                                 gu_row[0:S, :].rearrange("s (b n) -> s b n", b=8)).then_inc(s["seq_loaded"], 16)
                    after(sp, "hs_read", now)
                    sp.dma_start(hs_row[C:C + S, :].rearrange("s (b n) -> s b n", b=8), hs[:, 0:2 * LN]
                                 ).then_inc(s["hs_loaded"], 16)
                    back = v_hs[C + S:128, :].rearrange("s (i b n) -> s i b n", i=NP, b=8)
                    for i in range(NP):
                        at = 2 * LN + i * 2 * W
                        sp.dma_start(back[:, i, :, :], hs[:, at:at + 2 * W]).then_inc(s["hs_loaded"], 16)
                    if first + 1 < PAIRS:
                        after(sp, "x0v0_done", now)
                        sp.dma_start(x0[:, :], x[:, bass.ds(x_next, N)]).then_inc(s["x_loaded"], 16)
                if l3b:
                    after(sp, "x_out_done", done3)
                    sp.dma_start(out[:, bass.ds(stored_at, N)], x_out[:, :]).then_inc(s["stored"], 16)

            for k in range(FILL):
                step(k, k)
            with sp.Fori(FILL, PAIRS - 1) as k:
                step(k, FILL)
            for k in range(PAIRS - 1, STEPS):
                step(k, k)
            sp.wait_ge(s["stored"], 16 * PAIRS)

        @block.tensor
        def _(pe):
            mm = nc.tensor.matmul
            pe.wait_ge(s["weights_in"], 16)
            def gn_product(a, b, event, p_gn=p_gn):
                n = (b - a) * NP * 2
                mm(p_gn[0:C, 0:n], w("group", 0, C),
                   stats[:, a:b, :, :].rearrange("p a i (f t) -> p (a i f) t", f=2)[:, :, 1], start=True, stop=True)
                mm(p_gn[0:C, n:2 * n], w("group", 0, C), halves[:, a:b, :, :].rearrange("p a i f -> p (a i f)"),
                   start=True, stop=True).then_inc(s[event], 1)

            mm(bank[0][0:32, 0:32], w("vt", 0, 16), w("ut", 0, 16), start=True, stop=True).then_inc(s["setup_pe"], 1)
            mm(bank[1][0:32, 0:32], w("ut", 0, 16), w("vt", 0, 16), start=True, stop=True).then_inc(s["setup_pe"], 1)
            for r, k in enumerate((1, 2, 4, 8)):
                n = min(k, 15 - k)
                after(pe, "powers_done", 2 * (r + 1))
                mm(bank[0][0:32, 0:n * 32], pw_b[:, k - 1, :], pw_a[:, 0:n, :], start=True, stop=True
                   ).then_inc(s["setup_pe"], 1)
                if k < 8:
                    mm(bank[1][0:32, 0:k * 32], pw_a[:, k - 1, :], pw_b[:, 0:k, :], start=True, stop=True
                       ).then_inc(s["setup_pe"], 1)
                if k == 1:
                    mm(bank[4][:, 0:C], w("expand", 0, NF), w("filt", 0, NF), start=True, stop=True)
                    mm(bank[3][:, 0:GR], w("nb", 0, C).broadcast_to([C, 128]), w("g1", 0, C), start=True, stop=True)
                    after(pe, "gn1_done", 1)
                    mm(bank[2][0:C, 0:GR], w("ones", 0, C), gn1[:, :], start=True, stop=True).then_inc(s["setup_pe"], 1)
                if k == 2:
                    after(pe, "gn0_e2", 1)
                    gn_product(0, 1, "gn0_group", bank[5])
            after(pe, "setup_dve", 1)
            after(pe, "setup_pool", 1)

            def step(k, first):
                l0, l1, l2a, l2b, l3a, l3b = active(first)
                gn = gn_range(first)
                if l0 and first > 0:
                    after(pe, "gn_moments", k - 1)
                    after(pe, "spec_ready", k - 4)
                    after(pe, "gn0_e2", k + 1)
                    gn_product(0, 1, "gn0_group")
                if l2b:
                    j = k - 3
                    after(pe, "xw_done", j + 1)
                    after(pe, "xw_pool_done", j + 1)
                    convolution(0)
                if l0:
                    j = k
                    after(pe, "v0_ready", j + 1)
                    after(pe, "d_read", j)
                    mm(p_proj[0:64, :], w("proj", 0, C), v0, start=True, stop=True).then_inc(s["proj_done"], 1)
                    after(pe, "hs_read", j)
                    for c in range(2 * NP):
                        mm(p_h[:, c, :], v0[:, c * HALF:(c + 1) * HALF], w("ln", 0, C), start=True, stop=True)
                if gn:
                    after(pe, "spec_ready", k - 4)
                    after(pe, "gn0_moments", k + 1)
                    after(pe, "gn_e2", k)
                    gn_product(*gn, "gn_group")
                if l0:
                    j = k
                    after(pe, "v0sq_done", j + 1)
                    for c in range(2 * NP):
                        last = mm(p_ssq[:, c:c + 1], v0sq[:, c * HALF:(c + 1) * HALF], w("ones", 0, C)[:, 0:1],
                                  start=True, stop=True)
                    last.then_inc(s["ssq_done"], 1)
                if l2b:
                    convolution(1).then_inc(s["conv2_done"], 1)
                if l2a:
                    after(pe, "v2_ready", k - 1)
                    after(pe, "y_pix_done", k - 2)
                    for ci in range(2):
                        for i in range(NP):
                            at = i * PIX + ci * HALF
                            o = (ci * NP + i) * C
                            last = nc.tensor.transpose(p_xt[:, o:o + C], v2[:, at:at + HALF], w("ident", 0, C)[:, 0:C])
                    last.then_inc(s["xt_done"], 1)
                if l3a:
                    j = k - 4
                    after(pe, "v3_ready", j + 1)
                    after(pe, "tpad_done", j)
                    for c in range(2 * NP):
                        last = mm(p_t[:, c * C:(c + 1) * C], v3[:, c * HALF:(c + 1) * HALF], w("win3", 0, C),
                                  start=True, stop=True)
                    last.then_inc(s["t_done"], 1)
                if l0:
                    j = k
                    after(pe, "h1_pix_done", j + 1)
                    after(pe, "gelu1_done", k - 1)
                    for c in range(2 * NP):
                        last = nc.tensor.transpose(p_h1[0:GR, c * HALF:(c + 1) * HALF], h1_pix[:, c, :], w("ident"))
                    last.then_inc(s["h1_back_done"], 1)
                    if first == 0:
                        pe.wait_ge(s["toep_ready"], 1)
                    after(pe, "seq_loaded", 32 * (j + 1))
                    after(pe, "h_scaled_done", j + 1)
                    for m in range(2):
                        for mo in range(2):
                            for ci in range(2):
                                lhs = toep[:, m, ci, mo * 128:(mo + 1) * 128]
                                if m == 0:
                                    dst = p_toep[:, mo * LN:(mo + 1) * LN]
                                else:
                                    dst = p_toep[:, 2 * LN:4 * LN].rearrange("p (i a w) -> p a i w", i=NP, a=2)[:, mo]
                                last = mm(dst, lhs, seq[:, m, ci, :], start=ci == 0, stop=ci == 1)
                    last.then_inc(s["toep_done"], 1)
                if l3a:
                    j = k - 4
                    after(pe, "t_pix_done", j + 1)
                    after(pe, "gn_moments", k)
                    mm(p_spec[:, 0:2 * NP * C], w("dft"), t_pix[:, :, :].rearrange("p a b -> p (a b)"),
                       start=True, stop=True).then_inc(s["spec_done"], 1)
                if l2b:
                    j = k - 3
                    after(pe, "x3_done", j)
                    after(pe, "y_pix_done", j + 1)
                    for i in range(NP):
                        for co in range(2):
                            at = i * PIX + co * HALF
                            last = nc.tensor.transpose(p_back[0:C, at:at + HALF], y_pix[:, co, i, :], w("ident"))
                    last.then_inc(s["back_done"], 1)
                if l0:
                    j = k
                    after(pe, "h1_done", j + 1)
                    mm(p_gate[0:C, :], w("g2", 0, GR), h1[:, :], start=True, stop=True).then_inc(s["gate_done"], 1)
                if l3a:
                    j = k - 4
                    after(pe, "spec_ready", j + 1)
                    for c in range(2 * NP):
                        last = mm(p_inv[0:CP, c * HALF:(c + 1) * HALF], spec[:, c, :], w("idft"), start=True, stop=True)
                    last.then_inc(s["inv_done"], 1)
                if l3b:
                    j = k - 5
                    after(pe, "prod3_done", j + 1)
                    after(pe, "x_out_done", j)
                    mm(p_out[0:C, :], w("wout3", MID, CP), prod3[MID:CP, :], start=True, stop=True
                       ).then_inc(s["out_done"], 1)
                if l0:
                    j = k
                    after(pe, "hs_ready", j + 1)
                    after(pe, "hs_loaded", 48 * (j + 1))
                    after(pe, "proj_read", j + 1)
                    mm(p_d[0:C, :], dlhs, v_hs[:, :], start=True, stop=True).then_inc(s["d_done"], 1)
                if l1:
                    j = k - 1
                    after(pe, "v1_ready", j + 1)
                    after(pe, "tanh_gate_done", k + 1)
                    mm(p_l1[0:C, :], w12[:, :], v1[:, :], start=True, stop=False)
                    after(pe, "max_done", j + 1)
                    mm(p_l1[0:C, :], w("w2", 0, C), max_all[:, :], start=False, stop=True).then_inc(s["l1_done"], 1)

            def convolution(co):
                for i, (n, ci) in enumerate([(n, ci) for n in range(NPT) for ci in range(2)]):
                    q = P8 * (1 + co - ci)
                    last = mm(p_conv[:, co * NP * C:(co + 1) * NP * C],
                              bumps[:, n, q:q + P8, :].rearrange("p a b -> p (a b)"),
                              xw[:, n, ci, :, :].rearrange("p a b -> p (a b)"),
                              start=i == 0, stop=i == 2 * NPT - 1)
                return last

            for k in range(FILL):
                step(k, k)
            with pe.Fori(FILL, PAIRS) as k:
                step(k, FILL)
            for k in range(PAIRS, STEPS):
                step(k, k)

        @block.scalar
        def _(act):
            f = nc.scalar.activation
            act.wait_ge(s["weights_in"], 16)
            f(sig_a[:, 0:1], w("alog", 0, 32), ACT.Tanh, scale=0.5).then_inc(s["setup_act"], 1)

            def step(k, first):
                l0, l1, l2a, l2b, l3a, l3b = active(first)
                if l3b:
                    j = k - 5
                    after(act, "tpad_done", j + 1)
                    after(act, "two_taps_done", j)
                    taps = w("wdw", 0, CP)
                    f(tap_a[:, :, :], tpad[:, 0:ROWS, 0:W], ACT.Copy, scale=taps[:, 0:1])
                    f(tap_b[:, :, :], tpad[:, 0:ROWS, 1:1 + W], ACT.Copy, scale=taps[:, 1:2]
                      ).then_inc(s["taps_ab_done"], 1)
                if l0:
                    j = k
                    after(act, "gn0_shift", j + 1)
                    after(act, "d_done", j)
                    after(act, "x0v0_done", j)
                    for i in range(NP):
                        at = slice(i * PIX, (i + 1) * PIX)
                        last = f(v0[:, at], x0[:, at], ACT.Identity, bias=shift[:, 0, i:i + 1], scale=rstd[:, 0, i:i + 1])
                    last.then_inc(s["v0_ready"], 1)
                    after(act, "v0_ready", j + 1)
                    after(act, "ssq_done", j)
                    f(v0sq[:, :], v0, ACT.Square).then_inc(s["v0sq_done"], 1)
                    after(act, "proj_done", j + 1)
                    after(act, "gu_done", j)
                    hiw = "p (h i w) -> p i h w"
                    f(tanh_g[:, :].rearrange(hiw, i=NP, w=W), img(p_proj, 32, 64), ACT.Tanh, bias=w("bg", 0, 32),
                      scale=0.5)
                    f(u_half[:, :].rearrange(hiw, i=NP, w=W), img(p_proj, 0, 32), ACT.Identity, bias=w("bin", 0, 32)
                      ).then_inc(s["proj_read"], 1)
                    after(act, "ssq_done", j + 1)
                    after(act, "ln_var_done", j)
                    f(ln_msq[:, :], p_h[:, :, GR], ACT.Square).then_inc(s["ln_msq_done"], 1)
                    after(act, "gu_done", j + 1)
                    after(act, "seq_loaded", 32 * j)
                    f(gu_row[0:S, :].rearrange("p (w i h) -> p i h w", i=NP, h=H),
                      gu_col[0:S, :].rearrange("p (h i w) -> p i h w", i=NP, w=W), ACT.Copy
                      ).then_inc(s["gu_row_done"], 1)
                if l3a:
                    j = k - 4
                    after(act, "gn_shift", k)
                    after(act, "t_done", j)
                    for i in range(NP):
                        at = slice(i * PIX, (i + 1) * PIX)
                        last = f(v3[:, at], x3[:, at], ACT.Identity, bias=shift[:, 3, i:i + 1], scale=rstd[:, 3, i:i + 1])
                    last.then_inc(s["v3_ready"], 1)
                if l2b:
                    j = k - 3
                    after(act, "conv2_done", j + 1)
                    after(act, "back_done", j)
                    f(y_pix[:, :, :, :].rearrange("p a b c -> p (a b c)"), p_conv[:, 0:2 * NP * C], ACT.Copy
                      ).then_inc(s["y_pix_done"], 1)
                if l2a:
                    j = k - 2
                    after(act, "xt_done", j + 1)
                    after(act, "xw_done", j)
                    after(act, "xw_pool_done", j)
                    f(x_pix[:, :, :].rearrange("p a b -> p (a b)"), p_xt[:, 0:2 * NP * C], ACT.Copy
                      ).then_inc(s["x_pix_done"], 1)
                if l0:
                    j = k
                    after(act, "h_in_done", j + 1)
                    after(act, "h1_back_done", j)
                    f(h1_pix[:, :, :], h_in[:, :, :], ACT.Gelu).then_inc(s["h1_pix_done"], 1)
                if l3a:
                    j = k - 4
                    after(act, "t_done", j + 1)
                    after(act, "spec_done", j)
                    f(t_pix[:, :, :].rearrange("p a b -> p (a b)"), p_t[:, 0:2 * NP * C], ACT.Copy
                      ).then_inc(s["t_pix_done"], 1)
                if l0:
                    j = k
                    after(act, "h1_back_done", j + 1)
                    after(act, "gate_done", j)
                    f(h1[:, :], p_h1[0:GR, :], ACT.Copy).then_inc(s["h1_done"], 1)
                    after(act, "toep_done", j + 1)
                    after(act, "hs_loaded", 48 * j)
                    f(hs[:, :], p_toep[:, 0:4 * LN], ACT.Copy
                      ).then_inc(s["hs_read"], 1)
                if l3b:
                    j = k - 5
                    after(act, "tap_done", 7 * (j + 1))
                    after(act, "prod3_done", j)
                    g = img(gelu3, MID, CP)
                    for i in range(NP):
                        last = f(g[:, i, :, :], conv[0:HID2, i * HP:i * HP + H, :], ACT.Gelu)
                    last.then_inc(s["gelu3_done"], 1)
                if l0:
                    j = k
                    after(act, "gate_done", j + 1)
                    after(act, "gated_done", j)
                    f(tanh_gate[:, :], p_gate[0:C, :], ACT.Tanh, bias=w("g2b", 0, C), scale=0.5
                      ).then_inc(s["tanh_gate_done"], 1)
                if l3a:
                    j = k - 4
                    after(act, "inv_done", j + 1)
                    after(act, "tap_done", 7 * j)
                    f(tpad[:, 1:1 + NP * HP, 1:1 + W].rearrange("p (i h) w -> p i h w", i=NP)[:, :, 0:H, :],
                      img(p_inv, 0, CP), ACT.Copy).then_inc(s["tpad_done"], 1)
                if l0:
                    j = k
                    after(act, "hs_loaded", 48 * (j + 1))
                    after(act, "d_done", j)
                    f(v_hs[C:C + S, :].rearrange("p (i h w) -> p i h w", i=NP, h=H),
                      hs_row[C:C + S, :].rearrange("p (w i h) -> p i h w", i=NP, h=H), ACT.Copy
                      ).then_inc(s["hs_ready"], 1)
                    after(act, "d_done", j + 1)
                    after(act, "gated_done", j)
                    f(d_half[:, :], p_d[0:C, :], ACT.Identity, bias=dbias[:, :]).then_inc(s["d_read"], 1)
                if l3a:
                    j = k - 4
                    after(act, "x3_done", j + 1)
                    after(act, "x_out_done", j)
                    f(x3_late[:, :], x3[:, :], ACT.Copy).then_inc(s["x3_late_done"], 1)
                if l1:
                    j = k - 1
                    after(act, "l1_done", j + 1)
                    after(act, "x2_done", j)
                    f(gelu1[:, :], p_l1[0:C, :], ACT.Gelu, bias=bnb[:, :], scale=bns[:, :]).then_inc(s["gelu1_done"], 1)
                if l2a:
                    j = k - 2
                    after(act, "x2_done", j + 1)
                    after(act, "x3_done", j)
                    f(x2_late[:, :], x2[:, :], ACT.Copy).then_inc(s["x2_late_done"], 1)

            for k in range(FILL):
                step(k, k)
            with act.Fori(FILL, PAIRS) as k:
                step(k, FILL)
            for k in range(PAIRS, STEPS):
                step(k, k)

        @block.gpsimd
        def _(pool):
            tt = nc.gpsimd.tensor_tensor
            nc.gpsimd.memset(tpad[:, :, :], 0.0)
            nc.gpsimd.memset(spec[:, :, HID2:MID], 0.0).then_inc(s["setup_pool"], 1)
            pool.wait_ge(s["weights_in"], 16)
            nc.gpsimd.tensor_scalar(bnv[:, :], w("var", 0, C), BN_EPS, None, ALU.add).then_inc(s["setup_pool"], 1)
            pool.wait_ge(s["setup_pool"], 2)
            tt(bnr[:, :], bnv[:, :], w("mhalf", 0, C)[:, 0:1], ALU.pow).then_inc(s["setup_pool"], 1)

            def norm_factors(a, b, moments_done, neg, var, powered, shifted, n, free):
                q = "p a i -> p (a i)"
                m = (b - a) * NP
                pool.wait_ge(s[moments_done], n)
                free()
                tt(neg_mean[:, a:b, :].rearrange(q), moments[:, 0, a:b, :].rearrange(q), w("mone", 0, C)[:, 0:m],
                   ALU.mult).then_inc(s[neg], 1)
                pool.wait_ge(s[var], n)
                tt(rstd[:, a:b, :].rearrange(q), gvar[:, a:b, :].rearrange(q), w("mhalf", 0, C)[:, 0:m], ALU.pow
                   ).then_inc(s[powered], 1)
                pool.wait_ge(s[neg], n)
                pool.wait_ge(s[powered], n)
                tt(shift[:, a:b, :].rearrange(q), neg_mean[:, a:b, :].rearrange(q), rstd[:, a:b, :].rearrange(q),
                   ALU.mult).then_inc(s[shifted], 1)

            def step(k, first):
                l0, l1, l2a, l2b, l3a, l3b = active(first)
                gn = gn_range(first)
                if l0:
                    norm_factors(0, 1, "gn0_moments", "gn0_neg", "gn0_var", "gn0_rstd", "gn0_shift", k + 1,
                                 lambda: after(pool, "v0_ready", k))
                if l1:
                    j = k - 1
                    after(pool, "gated_done", j + 1)
                    after(pool, "x0v0_done", j + 1)
                    after(pool, "v1_ready", j)
                    after(pool, "x2_done", j)
                    tt(x1[:, :], x0v0[:, :], gated[:, :], ALU.add).then_inc(s["x1_done"], 1)
                if l3b:
                    j = k - 5
                    after(pool, "taps_ab_done", j + 1)
                    after(pool, "tap_done", 7 * j)
                    tt(two_taps[:, :, :], tap_a[:, :, :], tap_b[:, :, :], ALU.add).then_inc(s["two_taps_done"], 1)
                if gn:
                    def free():
                        after(pool, "v1_ready", k - 1)
                        after(pool, "v2_ready", k - 2)
                        after(pool, "v3_ready", k - 4)
                    norm_factors(*gn, "gn_moments", "gn_neg", "gn_var", "gn_rstd", "gn_shift", k, free)
                if l0:
                    j = k
                    after(pool, "ln_var_done", j + 1)
                    after(pool, "h_scaled_done", j)
                    tt(ln_rstd[:, :], ln_var[:, :], w("mhalf")[:, 0:2 * NP], ALU.pow
                       ).then_inc(s["ln_rstd_done"], 1)
                    after(pool, "v0_ready", j + 1)
                    after(pool, "x1_done", j)
                    tt(x0v0[:, :], x0[:, :], v0, ALU.add).then_inc(s["x0v0_done"], 1)
                if l2a:
                    j = k - 2
                    after(pool, "x_pix_done", j + 1)
                    after(pool, "conv2_done", j)
                    for n in XW_POOL:
                        last = tt(xw[:, n, :, :, :].rearrange("p a b c -> p (a b) c"), x_pix[:, :, :],
                                  w("wb")[:, n * C:(n + 1) * C].unsqueeze(1).broadcast_to([128, 2 * NP, C]), ALU.mult)
                    last.then_inc(s["xw_pool_done"], 1)
                if l1:
                    j = k - 1
                    after(pool, "gelu1_done", j + 1)
                    after(pool, "x1_done", j + 1)
                    after(pool, "v2_ready", j)
                    after(pool, "x2_late_done", j)
                    tt(x2[:, :], x1[:, :], gelu1[:, :], ALU.add).then_inc(s["x2_done"], 1)

            for k in range(FILL):
                step(k, k)
            with pool.Fori(FILL, PAIRS) as k:
                step(k, FILL)
            for k in range(PAIRS, STEPS):
                step(k, k)

        @block.vector
        def _(dve):
            tt, ts, stt = nc.vector.tensor_tensor, nc.vector.tensor_scalar, nc.vector.scalar_tensor_tensor
            copy = nc.vector.tensor_copy
            done = {}

            def link(ins, event="setup_steps"):
                done[event] = done.get(event, 0) + 1
                ins.then_inc(s[event], 1)
                dve.wait_ge(s[event], done[event])

            def half(t):
                return ts(t, t, 0.5, None, ALU.mult)

            def block_statistics(st):
                for i in range(NP):
                    last = nc.vector.bn_stats(stats[:, st, i, :], xs[st][:, i * PIX:(i + 1) * PIX])
                return last

            def statistics_end(a, b, events, n):
                dve.wait_ge(s[events[0]], n)
                t = stats[:, a:b, :, :].rearrange("p a i (f t) -> p (a i f) t", f=2)
                q = "p a i f -> p (a i f)"
                tt(squares[:, a:b, :, :].rearrange(q), t[:, :, 1], t[:, :, 1], ALU.mult).then_inc(s[events[1]], 1)
                dve.wait_ge(s[events[1]], n)
                stt(halves[:, a:b, :, :].rearrange(q), t[:, :, 2], 2.0 / PIX, squares[:, a:b, :, :].rearrange(q),
                    ALU.mult, ALU.add).then_inc(s[events[2]], 1)

            def group_variance(a, b, events, n, p_gn=p_gn):
                m = (b - a) * NP
                dve.wait_ge(s[events[0]], n)
                nc.vector.tensor_reduce(moments[:, :, a:b, :], p_gn[0:C, 0:4 * m].rearrange(
                    "p (q a i f) -> p q a i f", q=2, a=b - a, i=NP), AX.X, ALU.add).then_inc(s[events[1]], 1)
                dve.wait_ge(s[events[1]], n)
                tt(msq[:, a:b, :], moments[:, 0, a:b, :], moments[:, 0, a:b, :], ALU.mult).then_inc(s[events[2]], 1)
                dve.wait_ge(s[events[2]], n)
                q = "p a i -> p (a i)"
                stt(gvar[:, a:b, :].rearrange(q), moments[:, 1, a:b, :].rearrange(q), GN_EPS,
                    msq[:, a:b, :].rearrange(q), ALU.add, ALU.subtract).then_inc(s[events[3]], 1)

            dve.wait_ge(s["weights_in"], 16)
            at = cols["proj"][0]
            half(wt[0:C, at:at + 32])
            half(w("bin", 0, 32))
            half(w("bg", 0, 32))
            half(w("g2b", 0, C))
            link(ts(gn1[:, :], w("g1", 0, C), w("nw", 0, C), None, ALU.mult), "gn1_done")
            dve.wait_ge(s["setup_act"], 1)
            link(ts(sig_a[:, 1:2], sig_a[:, 0:1], 0.5, 0.5, ALU.mult, ALU.add))
            dve.wait_ge(s["setup_pe"], 2)
            stt(pw_a[:, 0, :], w("id32", 0, 32), sig_a[:, 1:2], bank[0][0:32, 0:32], ALU.mult, ALU.add
                ).then_inc(s["powers_done"], 1)
            stt(pw_b[:, 0, :], w("id32", 0, 32), sig_a[:, 1:2], bank[1][0:32, 0:32], ALU.mult, ALU.add
                ).then_inc(s["powers_done"], 1)
            got = 2

            def powers(k):
                nonlocal got
                got += 2 if k < 8 else 1
                dve.wait_ge(s["setup_pe"], got)
                n = min(k, 15 - k)
                last = copy(pw_a[:, k:k + n, :].rearrange("p a b -> p (a b)"), bank[0][0:32, 0:n * 32])
                if k < 8:
                    last.then_inc(s["powers_done"], 1)
                    last = copy(pw_b[:, k:k + k, :].rearrange("p a b -> p (a b)"), bank[1][0:32, 0:k * 32])
                last.then_inc(s["powers_done"], 1)

            link(tt(dsum[:, :], w("skr", 0, C), w("skc", 0, C), ALU.add))
            powers(1)
            got += 1
            stt(dlhs[0:C, :], dsum[:, :], 0.25, w("halfid", 0, C), ALU.mult, ALU.subtract)
            ts(dlhs[C:128, :], dlhs[C:128, :], 0.125, None, ALU.mult)
            dve.wait_ge(s["x_loaded"], 16)
            block_statistics(0).then_inc(s["gn0_stats"], 1)
            statistics_end(0, 1, ("gn0_stats", "gn0_sq", "gn0_e2"), 1)
            powers(2)
            link(nc.vector.tensor_reduce(dbias[:, :], w("dbias", 0, C), AX.X, ALU.add))
            group_variance(0, 1, ("gn0_group", "gn0_moments", "gn0_msq", "gn0_var"), 1, bank[5])
            powers(4)
            ts(dbias[:, :], dbias[:, :], 0.25, None, ALU.mult)
            tt(w("ln", 0, C)[:, 0:GR], gn1[:, :], bank[2][0:C, 0:GR], ALU.subtract)
            tt(hbias[:, :], w("g1b"), bank[3][:, 0:GR], ALU.add)
            powers(8)
            dve.wait_ge(s["powers_done"], 9)
            tt(strip[:, 16:31, :], pw_a[:, :, 0:S], pw_a[:, :, S:2 * S], ALU.add)
            tt(strip[:, 14::-1, :], pw_a[:, :, 0:S], pw_a[:, :, S:2 * S], ALU.add)
            link(tt(strip[:, 15, :], w("id32", 0, 32)[:, 0:S], w("id32", 0, 32)[:, S:2 * S], ALU.add))
            ts(strip[:, 15, :], strip[:, 15, :], 2.0, None, ALU.mult
               ).then_inc(s["strip_done"], 1)
            copy(filt[:, :], bank[4][:, 0:C]).then_inc(s["setup_dve"], 1)

            def toeplitz():
                dve.wait_ge(s["lines_loaded"], 64)
                for m in range(2):
                    for half in range(2):
                        last = copy(toep[:, m, half, :].rearrange("p (a s b) -> p a s b", a=2, b=8),
                                    lines[:, m, half, :].rearrange("p (b a s) -> p a s b", a=2, b=8))
                last.then_inc(s["toep_ready"], 1)

            def later_weights():
                tt(w12[:, :], w("w1", 0, C), w("w2", 0, C), ALU.subtract)
                dve.wait_ge(s["setup_pool"], 3)
                tt(bnd[:, :], w("cb", 0, C), w("mean", 0, C), ALU.subtract)
                link(tt(bns[:, :], bnr[:, :], w("gamma", 0, C), ALU.mult))
                stt(bnb[:, :], bnd[:, :], bns[:, :], w("beta", 0, C), ALU.mult, ALU.add)
                link(nc.vector.reciprocal(rinv[:, :], w("rad")))
                link(ts(nrinv[:, :], rinv[:, :], -1.0, None, ALU.mult))
                wc = w("wc")
                for n in range(NPT):
                    ts(axd[:, n, :], w("dx"), wc[:, 2 * n:2 * n + 1], None, ALU.subtract)
                    last = ts(ayd[:, n, :], w("dy"), wc[:, 2 * n + 1:2 * n + 2], None, ALU.add)
                link(last)
                stt(axa[:, :, :], axd[:, :, :], -1.0, axd[:, :, :], ALU.mult, ALU.max)
                link(stt(aya[:, :, :], ayd[:, :, :], -1.0, ayd[:, :, :], ALU.mult, ALU.max))
                for n in range(NPT):
                    stt(ax[:, n, :], axa[:, n, :], rinv[:, n:n + 1], w("bigx"), ALU.mult, ALU.add)
                    last = stt(ay[:, n, :], aya[:, n, :], nrinv[:, n:n + 1], w("oney"), ALU.mult, ALU.add)
                link(last)
                for n in range(NPT):
                    last = tt(graw[:, n, :, :], ay[:, n, :].unsqueeze(2).broadcast_to([128, WIN, W]),
                              ax[:, n, :].unsqueeze(1).broadcast_to([128, WIN, W]), ALU.subtract)
                link(last)
                link(ts(bumps[:, :, :, :].rearrange("p a b c -> p (a b c)"),
                        graw[:, :, :, :].rearrange("p a b c -> p (a b c)"), 0.0, None, ALU.max))

            def normalise(st):
                for i in range(NP):
                    at = slice(i * PIX, (i + 1) * PIX)
                    last = ts(vs[st][:, at], xs[st][:, at], moments[:, 0, st, i:i + 1], rstd[:, st, i:i + 1],
                              ALU.subtract, ALU.mult)
                return last

            def step(k, first):
                l0, l1, l2a, l2b, l3a, l3b = active(first)
                gn = gn_range(first)

                def taps3(first_tap, last_tap):
                    j = k - 5
                    taps = w("wdw", 0, CP)
                    for t in range(first_tap, last_tap):
                        src = tpad[:, t // 3:t // 3 + ROWS, t % 3:t % 3 + W]
                        so_far = two_taps if t == 2 else conv
                        if t > 2:
                            after(dve, "tap_done", 7 * j + t - 2)
                        stt(conv[:, :, :], src, taps[:, t:t + 1], so_far[:, :, :], ALU.mult, ALU.add
                            ).then_inc(s["tap_done"], 1)

                if l0 and first > 0:
                    dve.wait_ge(s["x_loaded"], 16 * (k + 1))
                    block_statistics(0).then_inc(s["gn0_stats"], 1)
                    statistics_end(0, 1, ("gn0_stats", "gn0_sq", "gn0_e2"), k + 1)
                if l1:
                    j = k - 1
                    after(dve, "tanh_gate_done", j + 1)
                    after(dve, "d_read", j + 1)
                    after(dve, "x1_done", j)
                    stt(gated[:, :], tanh_gate[:, :], 1.0, d_half[:, :], ALU.add, ALU.mult).then_inc(s["gated_done"], 1)
                if l0 and first > 0:
                    group_variance(0, 1, ("gn0_group", "gn0_moments", "gn0_msq", "gn0_var"), k + 1)
                if l3a:
                    after(dve, "x3_done", k - 3)
                    last = block_statistics(3)
                if l2a:
                    after(dve, "x2_done", k - 1)
                    last = block_statistics(2)
                if l1:
                    after(dve, "x1_done", k)
                    last = block_statistics(1)
                if gn:
                    last.then_inc(s["gn_stats"], 1)
                    statistics_end(*gn, ("gn_stats", "gn_sq", "gn_e2"), k)
                if l3b:
                    j = k - 5
                    after(dve, "tpad_done", j + 1)
                    after(dve, "two_taps_done", j + 1)
                    after(dve, "gelu3_done", j)
                    after(dve, "prod3_done", j)
                    taps3(2, 3)
                if gn:
                    group_variance(*gn, ("gn_group", "gn_moments", "gn_msq", "gn_var"), k)
                if l3b:
                    taps3(3, 4)
                    taps3(4, 5)
                if l0:
                    j = k
                    after(dve, "proj_read", j + 1)
                    after(dve, "gu_row_done", j)
                    after(dve, "seq_loaded", 32 * j)
                    stt(gu_col[:, :], tanh_g[:, :], 1.0, u_half[:, :], ALU.add, ALU.mult).then_inc(s["gu_done"], 1)
                    after(dve, "ssq_done", j + 1)
                    after(dve, "ln_msq_done", j + 1)
                    after(dve, "ln_rstd_done", j)
                    stt(ln_var[:, :], p_ssq, LN_EPS, ln_msq[:, :], ALU.add, ALU.subtract
                        ).then_inc(s["ln_var_done"], 1)
                if l1:
                    j = k - 1
                    after(dve, "gn_rstd", k)
                    after(dve, "l1_done", j)
                    after(dve, "horiz_done", j)
                    normalise(1).then_inc(s["v1_ready"], 1)
                if l3b:
                    taps3(5, 6)
                if l2a:
                    j = k - 2
                    after(dve, "gn_rstd", k)
                    after(dve, "xt_done", j)
                    normalise(2).then_inc(s["v2_ready"], 1)
                if l3b:
                    taps3(6, 7)
                if l0:
                    j = k
                    after(dve, "ln_rstd_done", j + 1)
                    after(dve, "h1_pix_done", j)
                    tt(h_scaled[:, :, :], p_h[:, :, 0:GR], ln_rstd[:, :].unsqueeze(2).broadcast_to([128, 2 * NP, GR]),
                       ALU.mult).then_inc(s["h_scaled_done"], 1)
                    after(dve, "h_scaled_done", j + 1)
                    tt(h_in[:, :, :], h_scaled[:, :, :], hbias[:, :].unsqueeze(1).broadcast_to([128, 2 * NP, GR]),
                       ALU.add).then_inc(s["h_in_done"], 1)
                if l3b:
                    taps3(7, 8)
                    taps3(8, 9)
                if l1:
                    j = k - 1
                    v, m1 = img(v1), img(max_v1)
                    after(dve, "v1_ready", j + 1)
                    after(dve, "max_done", j)
                    tt(m1[:, :, 0:H - 2, :], v[:, :, 0:H - 2, :], v[:, :, 2:H, :], ALU.max)
                    tt(m1[:, :, H - 2:H, :], v[:, :, H - 2:H, :], v[:, :, 0:2, :], ALU.max).then_inc(s["vert1_done"], 1)
                    v, m = img(v1), img(max_h)
                    tt(m[:, :, :, 2:W - 2], v[:, :, :, 0:W - 4], v[:, :, :, 4:W], ALU.max)
                    tt(m[:, :, :, 0:2], v[:, :, :, W - 2:W], v[:, :, :, 2:4], ALU.max)
                    tt(m[:, :, :, W - 2:W], v[:, :, :, W - 4:W - 2], v[:, :, :, 0:2], ALU.max
                       ).then_inc(s["horiz_done"], 1)
                if l3a:
                    j = k - 4
                    after(dve, "spec_done", j + 1)
                    after(dve, "inv_done", j)
                    z = bass.AP(tensor=spec[:, :, :].tensor, offset=spec[:, :, :].offset,
                                ap=[list(spec[:, :, :].ap[0]), [CP, 2 * NP], [MID, 2], [1, HID2]])
                    tt(z, p_spec[:, 0:2 * NP * C].rearrange("p (a b c) -> p a b c", b=2, c=HID2),
                       filt[:, :].rearrange("p (b c) -> p b c", b=2).unsqueeze(1).broadcast_to([128, 2 * NP, 2, HID2]),
                       ALU.mult).then_inc(s["spec_ready"], 1)
                if l3b:
                    j = k - 5
                    after(dve, "gelu3_done", j + 1)
                    after(dve, "tap_done", 7 * (j + 1))
                    after(dve, "out_done", j)
                    g, p = img(gelu3, MID, CP), img(prod3, MID, CP)
                    for i in range(NP):
                        last = tt(p[:, i, :, :], g[:, i, :, :], conv[MID:CP, i * HP:i * HP + H, :], ALU.mult)
                    last.then_inc(s["prod3_done"], 1)
                if l1:
                    j = k - 1
                    m1, m2 = img(max_v1), img(max_v2)
                    after(dve, "vert1_done", j + 1)
                    tt(m2[:, :, 2:H, :], m1[:, :, 2:H, :], m1[:, :, 0:H - 2, :], ALU.max)
                    tt(m2[:, :, 0:2, :], m1[:, :, 0:2, :], m1[:, :, H - 2:H, :], ALU.max).then_inc(s["vert2_done"], 1)
                    after(dve, "vert2_done", j + 1)
                    after(dve, "horiz_done", j + 1)
                    after(dve, "l1_done", j)
                    tt(max_all[:, :], max_v2[:, :], max_h[:, :], ALU.max).then_inc(s["max_done"], 1)
                if l3b:
                    j = k - 5
                    after(dve, "out_done", j + 1)
                    after(dve, "x3_late_done", j + 1)
                    after(dve, "stored", 16 * j)
                    tt(x_out[:, :], x3_late[:, :], p_out[0:C, :], ALU.add).then_inc(s["x_out_done"], 1)
                if l2a:
                    j = k - 2
                    after(dve, "x_pix_done", j + 1)
                    after(dve, "conv2_done", j)
                    for n in XW_DVE:
                        last = tt(xw[:, n, :, :, :].rearrange("p a b c -> p (a b) c"), x_pix[:, :, :],
                                  w("wb")[:, n * C:(n + 1) * C].unsqueeze(1).broadcast_to([128, 2 * NP, C]), ALU.mult)
                    last.then_inc(s["xw_done"], 1)
                if l2b:
                    j = k - 3
                    after(dve, "back_done", j + 1)
                    after(dve, "x2_late_done", j + 1)
                    after(dve, "v3_ready", j)
                    after(dve, "x3_late_done", j)
                    tt(x3[:, :], x2_late[:, :], p_back[0:C, :], ALU.add).then_inc(s["x3_done"], 1)

            step(0, 0)
            toeplitz()
            later_weights()
            for k in range(1, FILL):
                step(k, k)
            with dve.Fori(FILL, PAIRS) as k:
                step(k, FILL)
            for k in range(PAIRS, STEPS):
                step(k, k)


def packed_weights(a):
    cols, n = weight_layout()
    wt = np.zeros((128, n), np.float32)

    def put(name, value, p0=0, c0=0):
        value = np.asarray(value)
        if value.ndim == 1:
            value = value[:, None]
        at = cols[name][0] + c0
        wt[p0:p0 + value.shape[0], at:at + value.shape[1]] = value

    for name, value in shape_constants().items():
        put(name, value)
    put("ln", np.full((C, 1), 1.0 / C), c0=GR)
    for i, d in enumerate(("row", "col")):
        g = {key: a[f"L0_conv_{d}_{key}"] for key in ("a_logit", "U", "V", "Win", "bin", "Wg", "bg", "Wout", "bout",
                                                      "Wskip", "bskip")}
        put("proj", g["Win"].T, c0=i * S)
        put("proj", g["Wg"].T, c0=32 + i * S)
        put("bin", g["bin"], p0=i * S)
        put("bg", g["bg"], p0=i * S)
        put("alog", g["a_logit"], p0=i * S)
        put("vt", g["V"].T, p0=i * R, c0=i * S)
        put("ut", g["U"].T, p0=i * R, c0=i * S)
        put("skr" if i == 0 else "skc", g["Wskip"].T)
        put("dlhs", g["Wout"].T, p0=C + i * S)
        put("dbias", g["bout"], c0=2 * i)
        put("dbias", g["bskip"], c0=2 * i + 1)
    put("g1", a["L0_conv_g1_w"].T)
    put("g1b", np.broadcast_to(a["L0_conv_g1_b"].reshape(1, GR), (128, GR)))
    put("nw", a["L0_conv_norm_w"])
    put("nb", a["L0_conv_norm_b"])
    put("g2", a["L0_conv_g2_w"].T)
    put("g2b", a["L0_conv_g2_b"])
    put("w1", a["L1_conv_conv_w"][:, :C].T)
    put("w2", a["L1_conv_conv_w"][:, C:].T)
    for name, key in (("cb", "conv_b"), ("gamma", "bn_gamma"), ("beta", "bn_beta"), ("mean", "bn_mean"),
                      ("var", "bn_var")):
        put(name, a["L1_conv_" + key])
    put("wc", np.broadcast_to(a["L2_conv_weight_coord"].reshape(1, 2 * NPT), (128, 2 * NPT)))
    put("rad", np.broadcast_to(a["L2_conv_radius"].reshape(1, NPT), (128, NPT)))
    put("wb", np.broadcast_to(a["L2_conv_weights"][0].T.reshape(1, NPT * C), (128, NPT * C)))
    put("filt", a["L3_conv_fft_filter"].reshape(C, NF).T)
    put("win3", a["L3_conv_w_in"].T)
    put("wout3", a["L3_conv_w_out"].T, p0=MID)
    taps = a["L3_conv_w_dw"].reshape(C, 9)
    put("wdw", taps[:HID2])
    put("wdw", taps[HID2:], p0=MID)
    return wt


def kernel(**inputs):
    import concourse.bacc as bacc
    from concourse.bass_utils import run_bass_kernel_spmd

    a = {name: np.asarray(value) for name, value in inputs.items()}
    nc = bacc.Bacc("TRN2", target_bir_lowering=False, num_devices=1)
    arrays = {
        "x_channels": np.ascontiguousarray(a["x"].transpose(1, 0, 2, 3).reshape(C, B * PIX)),
        "weights_packed": packed_weights(a),
    }
    args = [nc.dram_tensor(name, v.shape, mybir.dt.from_np(v.dtype), kind="ExternalInput").ap()
            for name, v in arrays.items()]
    out = nc.dram_tensor("out_channels", (C, B * PIX), mybir.dt.float32, kind="ExternalOutput").ap()
    build(nc, *args, out)
    got = run_bass_kernel_spmd(nc, [arrays], core_ids=[0]).results[0]["out_channels"]
    return np.ascontiguousarray(got.reshape(C, B, H, W).transpose(1, 0, 2, 3))
```

```python
import numpy as np
import concourse.bass as bass
from concourse import mybir
from contextlib import ExitStack

B, C, H, W = 16, 96, 16, 16
S, R, GR = 16, 8, 16
NP = 2
PAIRS = B // NP
PIX = H * W
N = NP * PIX
HALF = PIX // 2
LN = H * NP
K2, PAD2, NPT = 11, 5, 4
P8 = 8
NF = P8 * (P8 // 2 + 1)
HID2 = C // 2
MID = 64
CP = MID + HID2
WP = W + 2
HP = H + 1
ROWS = NP * HP - 1
WIN = 3 * P8
BIG = 1e30
GN_EPS, LN_EPS, BN_EPS = 1e-5, 1e-6, 1e-5


STEPS = PAIRS + 5
XW_DVE, XW_POOL = (0, 1), (2, 3)
FILL = 6


def active(step):
    return tuple(age <= step < PAIRS + age for age in range(6))


def gn_range(step):
    on = [b for b, age in ((1, 1), (2, 2), (3, 4)) if age <= step < PAIRS + age]
    return (on[0], on[-1] + 1) if on else None


def weight_layout():
    cols, at = {}, 0
    for name, n in [("proj", 64), ("ln", GR + 1), ("group", C), ("ones", C), ("g1", GR), ("nw", 1), ("nb", 1), ("g1b", GR),
                    ("bin", 1), ("bg", 1), ("alog", 1), ("vt", 32), ("ut", 32), ("id32", 32), ("g2", C), ("g2b", 1),
                    ("skr", C), ("skc", C), ("halfid", C), ("dlhs", C), ("dbias", 4),
                    ("w1", C), ("w2", C), ("cb", 1), ("gamma", 1), ("beta", 1), ("mean", 1), ("var", 1),
                    ("wc", 2 * NPT), ("rad", NPT), ("dx", W), ("bigx", W), ("dy", WIN), ("oney", WIN), ("wb", NPT * C),
                    ("win3", C), ("wout3", C), ("wdw", 9), ("filt", C), ("expand", 128), ("dft", 128), ("idft", 128),
                    ("ident", 128), ("mhalf", 16), ("mone", 16)]:
        cols[name] = (at, n)
        at += n
    return cols, at


def shape_constants():
    c = {}
    c["group"] = np.kron(np.eye(32), np.ones((3, 3))) / 6.0
    c["ones"] = np.full((C, C), 1.0 / C)
    c["halfid"] = 0.5 * np.eye(C)
    c["id32"] = np.eye(32)
    c["ident"] = np.eye(128)
    c["mhalf"] = np.full((128, 16), -0.5)
    c["mone"] = np.full((128, 16), -1.0)
    yl, xi = np.divmod(np.arange(128), W)
    xo, q = np.arange(W), np.arange(-P8, 2 * P8)
    dx, dy = xi[:, None] - xo[None], yl[:, None] - q[None]
    c["dx"], c["dy"] = dx / PAD2, dy / PAD2
    c["bigx"] = np.where(np.abs(dx) <= PAD2, 0.0, BIG)
    c["oney"] = np.where(np.abs(dy) <= PAD2, 1.0, 1.0 - BIG)
    y, x = np.mgrid[0:P8, 0:P8]
    basis, expand = [], []
    for kx in range(P8 // 2 + 1):
        for ky in range(P8):
            own = np.zeros(NF)
            if kx in (0, P8 // 2):
                if ky > P8 // 2:
                    continue
                own[ky * 5 + kx] += 0.5
                own[(P8 - ky) % P8 * 5 + kx] += 0.5
            else:
                own[ky * 5 + kx] = 1.0
            angle = 2 * np.pi * (ky * y + kx * x) / P8
            if kx in (0, P8 // 2) and ky in (0, P8 // 2):
                basis.append(np.cos(angle) / P8)
                expand.append(own)
            else:
                basis += [np.sqrt(2) / P8 * np.cos(angle), np.sqrt(2) / P8 * np.sin(angle)]
                expand += [own, own]
    basis = np.array(basis)
    dft = np.zeros((P8, 2, P8, 2, 64))
    for b in range(2):
        dft[:, b, :, b, :] = basis.transpose(1, 2, 0)
    c["dft"] = dft.reshape(128, 128)
    c["idft"] = c["dft"].T
    c["expand"] = np.tile(np.array(expand).T, (1, 2))
    return c


def build(nc, x, wts, out):
    F32 = mybir.dt.float32
    ALU = mybir.AluOpType
    ACT = mybir.ActivationFunctionType
    AX = mybir.AxisListType
    cols, NW = weight_layout()

    ctx = ExitStack()
    with ctx:
        def sb(name, shape):
            return ctx.enter_context(nc.sbuf_tensor(name, shape, F32))

        def sem(name):
            return ctx.enter_context(nc.semaphore(name))

        wt = sb("weights", [128, NW])

        def w(name, p0=0, p1=128):
            at, n = cols[name]
            return wt[p0:p1, at:at + n]

        x0, x1, x2, x3 = (sb(f"x{i}", [C, N]) for i in range(4))
        x2_late, x3_late, x3_later = (sb(n, [C, N]) for n in ("x2_late", "x3_late", "x3_later"))
        x_out, x0v0 = sb("x_out", [C, N]), sb("x0v0", [C, N])
        v_hs = sb("v_hs", [128, N])
        v0 = v_hs[0:C, :]
        v1, v2, v3 = (sb(f"v{i}", [C, N]) for i in range(1, 4))
        xs, vs = [x0, x1, x2, x3], [v0, v1, v2, v3]
        stats = sb("stats", [C, 4, NP, 6])
        halves = sb("halves", [C, 4, NP, 2])
        squares = sb("squares", [C, 4, NP, 2])
        moments = sb("moments", [C, 2, 4, NP])
        msq = sb("msq", [C, 4, NP])
        gvar = sb("gvar", [C, 4, NP])
        rstd = sb("rstd", [C, 4, NP])
        neg_mean, shift = sb("neg_mean", [C, 4, NP]), sb("shift", [C, 4, NP])
        v0sq = sb("v0sq", [C, N])
        tanh_g, u_half = sb("tanh_g", [32, N]), sb("u_half", [32, N])
        ln_msq, ln_var, ln_rstd = (sb(n, [128, 2 * NP]) for n in ("ln_msq", "ln_var", "ln_rstd"))
        gu_col = sb("gu_col", [32, N])
        gu_row = sb("gu_row", [32, N])
        seq = sb("seq", [128, 2, 2, LN])
        hs = sb("hs", [128, 4 * LN])
        hs_row = sb("hs_row", [128, N])
        h_scaled, h_in, h1_pix = (sb(n, [128, 2 * NP, GR]) for n in ("h_scaled", "h_in", "h1_pix"))
        h1 = sb("h1", [GR, N])
        tanh_gate, d_half, gated = sb("tanh_gate", [C, N]), sb("d_half", [C, N]), sb("gated", [C, N])
        max_v1, max_v2, max_h, max_all = (sb(f"max{i}", [C, N]) for i in range(4))
        gelu1 = sb("gelu1", [C, N])
        bumps = sb("bumps", [128, NPT, WIN, W])
        x_pix = sb("x_pix", [128, 2 * NP, C])
        xw = sb("xw", [128, NPT, 2, NP, C])
        y_pix = sb("y_pix", [128, 2, NP, C])
        t_pix = sb("t_pix", [128, 2 * NP, C])
        filt = sb("filt_spec", [128, C])
        spec = sb("spec", [128, 2 * NP, CP])
        tpad = sb("tpad", [CP, NP * HP + 1, WP])
        tap_a, tap_b, two_taps = (sb(n, [CP, ROWS, W]) for n in ("tap_a", "tap_b", "two_taps"))
        conv = sb("conv", [CP, ROWS, W])
        gelu3, prod3 = sb("gelu3", [CP, N]), sb("prod3", [CP, N])
        gn1, hbias = sb("gn1", [C, GR]), sb("hbias", [128, GR])
        dlhs = w("dlhs")
        dsum, dbias = sb("dsum", [C, C]), sb("dbias_half", [C, 1])
        w12, bnv, bnr, bns, bnd, bnb = sb("w12", [C, C]), *(sb(f"bn{i}", [C, 1]) for i in range(5))
        sig_a = sb("sig_a", [32, 2])
        pw_a, pw_b = sb("pw_a", [32, 15, 32]), sb("pw_b", [32, 8, 32])
        strip = sb("strip", [32, 31, S])
        lines = sb("lines", [128, 2, 2, 256])
        toep = sb("toep", [128, 2, 2, 256])
        rinv, nrinv = sb("rinv", [128, NPT]), sb("nrinv", [128, NPT])
        axd, ax = sb("axd", [128, NPT, W]), sb("ax", [128, NPT, W])
        ayd, ay = sb("ayd", [128, NPT, WIN]), sb("ay", [128, NPT, WIN])
        axa, aya = sb("axa", [128, NPT, W]), sb("aya", [128, NPT, WIN])
        graw = sb("graw", [128, NPT, WIN, W])

        bank = [ctx.enter_context(nc.psum_tensor(f"bank{i}", [128, 512], F32)) for i in range(8)]
        p_gn, p_spec = bank[0], bank[0]
        p_proj = bank[1]
        p_ln, p_toep = bank[2], bank[2]
        p_h, p_ssq = p_ln[:, 0:2 * NP * (GR + 1)].rearrange("p (a b) -> p a b", a=2 * NP), p_ln[:, 128:128 + 2 * NP]
        p_l1, p_h1, p_gate = bank[3], bank[3], bank[3]
        p_conv, p_xt = bank[4], bank[4]
        p_d = bank[5]
        p_t, p_inv = bank[6], bank[6]
        p_back, p_out = bank[7], bank[7]

        names = """weights_in x_loaded gn0_stats gn0_sq gn0_e2 gn0_group gn0_moments gn0_msq gn0_var gn0_neg gn0_rstd
        gn0_shift gn_stats gn_sq gn_e2 gn_group gn_moments gn_msq gn_var gn_neg gn_rstd gn_shift
        v0_ready v1_ready v2_ready v3_ready
        proj_done v0sq_done ssq_done proj_read gu_done gu_row_done seq_loaded toep_done hs_read hs_loaded hs_ready
        ln_msq_done ln_var_done ln_rstd_done h_scaled_done h_in_done h1_pix_done h1_back_done h1_done gate_done
        tanh_gate_done d_from_v_done d_done d_read gated_done x0v0_done x1_done
        vert1_done vert2_done horiz_done max_done l1_done gelu1_done x2_done x2_late_done
        xt_done x_pix_done xw_done xw_pool_done conv2_done y_pix_done back_done x3_done x3_late_done x3_later_done
        t_done t_pix_done spec_done spec_ready inv_done tpad_done taps_ab_done two_taps_done tap_done
        gelu3_done prod3_done out_done x_out_done stored
        setup_pe setup_dve setup_act setup_pool powers_done strip_done gn1_done setup_steps lines_loaded toep_ready""".split()
        s = {n: sem(n) for n in names}
        per_pair = {"x_loaded": 16, "seq_loaded": 32, "hs_loaded": 48, "tap_done": 7, "stored": 16}

        def after(eng, name, count):
            if isinstance(count, int):
                if not name.startswith(("gn_", "setup", "powers")):
                    count = min(count, PAIRS * per_pair.get(name, 1))
                if count <= 0:
                    return
            eng.wait_ge(s[name], count)

        def img(t, p0=0, p1=None):
            return t[p0:p1, :].rearrange("p (i h w) -> p i h w", i=NP, h=H)

        block = ctx.enter_context(nc.Block())

        @block.sync
        def _(sp):
            sp.dma_start(wt[:, :], wts).then_inc(s["weights_in"], 16)
            sp.dma_start(x0[:, :], x[:, 0:N]).then_inc(s["x_loaded"], 16)
            sp.wait_ge(s["strip_done"], 1)
            for m in range(2):
                for half in range(2):
                    first = strip[m * S:(m + 1) * S, :, :]
                    rows = bass.AP(tensor=first.tensor, offset=first.offset + (15 - half) * S,
                                   ap=[list(first.ap[0]), [-2 * S, 8], [1, 256]])
                    sp.dma_start(lines[:, m, half, :], rows).then_inc(s["lines_loaded"], 16)

            def step(k, first):
                l0, l3b = first < PAIRS, first >= 5
                value = (lambda v: v) if isinstance(k, int) else sp.snap
                now = value(k + 1)
                if l0 and first + 1 < PAIRS:
                    x_next = value((k + 1) * N)
                if l3b:
                    done3, stored_at = value(k - 4), value((k - 5) * N)
                if l0:
                    sp.wait_ge(s["gu_done"], now)
                    after(sp, "toep_done", k)
                    sp.dma_start(seq[:, 1, :, :].rearrange("p a n -> p (a n)"),
                                 gu_col[S:2 * S, :].rearrange("s (b n) -> s b n", b=8)).then_inc(s["seq_loaded"], 16)
                    sp.wait_ge(s["gu_row_done"], now)
                    sp.dma_start(seq[:, 0, :, :].rearrange("p a n -> p (a n)"),
                                 gu_row[0:S, :].rearrange("s (b n) -> s b n", b=8)).then_inc(s["seq_loaded"], 16)
                    if first + 1 < PAIRS:
                        sp.wait_ge(s["x0v0_done"], now)
                        sp.dma_start(x0[:, :], x[:, bass.ds(x_next, N)]).then_inc(s["x_loaded"], 16)
                    sp.wait_ge(s["hs_read"], now)
                    sp.dma_start(hs_row[C:C + S, :].rearrange("s (b n) -> s b n", b=8), hs[:, 0:2 * LN]
                                 ).then_inc(s["hs_loaded"], 16)
                    back = v_hs[C + S:128, :].rearrange("s (i b n) -> s i b n", i=NP, b=8)
                    for i in range(NP):
                        at = 2 * LN + i * 2 * W
                        sp.dma_start(back[:, i, :, :], hs[:, at:at + 2 * W]).then_inc(s["hs_loaded"], 16)
                if l3b:
                    sp.wait_ge(s["x_out_done"], done3)
                    sp.dma_start(out[:, bass.ds(stored_at, N)], x_out[:, :]).then_inc(s["stored"], 16)

            for k in range(FILL):
                step(k, k)
            with sp.Fori(FILL, PAIRS - 1) as k:
                step(k, FILL)
            for k in range(PAIRS - 1, STEPS):
                step(k, k)
            sp.wait_ge(s["stored"], 16 * PAIRS)

        @block.tensor
        def _(pe):
            mm = nc.tensor.matmul
            pe.wait_ge(s["weights_in"], 16)
            def gn_product(a, b, event, p_gn=p_gn):
                n = (b - a) * NP * 2
                mm(p_gn[0:C, 0:n], w("group", 0, C),
                   stats[:, a:b, :, :].rearrange("p a i (f t) -> p (a i f) t", f=2)[:, :, 1], start=True, stop=True)
                mm(p_gn[0:C, n:2 * n], w("group", 0, C), halves[:, a:b, :, :].rearrange("p a i f -> p (a i f)"),
                   start=True, stop=True).then_inc(s[event], 1)

            mm(bank[0][0:32, 0:32], w("vt", 0, 16), w("ut", 0, 16), start=True, stop=True).then_inc(s["setup_pe"], 1)
            mm(bank[1][0:32, 0:32], w("ut", 0, 16), w("vt", 0, 16), start=True, stop=True).then_inc(s["setup_pe"], 1)
            for r, k in enumerate((1, 2, 4, 8)):
                n = min(k, 15 - k)
                pe.wait_ge(s["powers_done"], 2 * (r + 1))
                mm(bank[0][0:32, 0:n * 32], pw_b[:, k - 1, :], pw_a[:, 0:n, :], start=True, stop=True
                   ).then_inc(s["setup_pe"], 1)
                if k < 8:
                    mm(bank[1][0:32, 0:k * 32], pw_a[:, k - 1, :], pw_b[:, 0:k, :], start=True, stop=True
                       ).then_inc(s["setup_pe"], 1)
                if k == 1:
                    mm(bank[4][:, 0:C], w("expand", 0, NF), w("filt", 0, NF), start=True, stop=True)
                    mm(bank[3][:, 0:GR], w("nb", 0, C).broadcast_to([C, 128]), w("g1", 0, C), start=True, stop=True)
                    pe.wait_ge(s["gn1_done"], 1)
                    mm(bank[2][0:C, 0:GR], w("ones", 0, C), gn1[:, :], start=True, stop=True).then_inc(s["setup_pe"], 1)
                if k == 2:
                    pe.wait_ge(s["gn0_e2"], 1)
                    gn_product(0, 1, "gn0_group", bank[5])
            pe.wait_ge(s["setup_dve"], 1)
            pe.wait_ge(s["setup_pool"], 1)

            def first_norm_means(k):
                after(pe, "gn_moments", k - 1)
                after(pe, "spec_ready", k - 4)
                pe.wait_ge(s["gn0_e2"], k + 1)
                gn_product(0, 1, "gn0_group")

            def change0_from_states(k):
                j = k
                pe.wait_ge(s["hs_ready"], j + 1)
                pe.wait_ge(s["hs_loaded"], 48 * (j + 1))
                mm(p_d[0:C, :], dlhs[C:128, :], v_hs[C:128, :], start=False, stop=True).then_inc(s["d_done"], 1)

            def project(k):
                j = k
                pe.wait_ge(s["v0_ready"], j + 1)
                after(pe, "proj_read", j)
                mm(p_proj[0:64, :], w("proj", 0, C), v0, start=True, stop=True).then_inc(s["proj_done"], 1)
                after(pe, "hs_read", j)
                for c in range(2 * NP):
                    mm(p_h[:, c, :], v0[:, c * HALF:(c + 1) * HALF], w("ln", 0, C), start=True, stop=True)

            def mean_squares(k):
                j = k
                pe.wait_ge(s["v0sq_done"], j + 1)
                for c in range(2 * NP):
                    last = mm(p_ssq[:, c:c + 1], v0sq[:, c * HALF:(c + 1) * HALF], w("ones", 0, C)[:, 0:1],
                              start=True, stop=True)
                last.then_inc(s["ssq_done"], 1)

            def transpose_convolved(k):
                j = k - 3
                after(pe, "x3_done", j)
                after(pe, "x_out_done", j - 2)
                pe.wait_ge(s["y_pix_done"], j + 1)
                for i in range(NP):
                    for co in range(2):
                        at = i * PIX + co * HALF
                        last = nc.tensor.transpose(p_back[0:C, at:at + HALF], y_pix[:, co, i, :], w("ident"))
                last.then_inc(s["back_done"], 1)

            def norm_means(k, gn):
                after(pe, "spec_ready", k - 4)
                after(pe, "gn0_moments", k + 1)
                pe.wait_ge(s["gn_e2"], k)
                gn_product(*gn, "gn_group")

            def transpose_v2(k):
                after(pe, "v2_ready", k - 1)
                after(pe, "y_pix_done", k - 2)
                for ci in range(2):
                    for i in range(NP):
                        at = i * PIX + ci * HALF
                        o = (ci * NP + i) * C
                        last = nc.tensor.transpose(p_xt[:, o:o + C], v2[:, at:at + HALF], w("ident", 0, C)[:, 0:C])
                last.then_inc(s["xt_done"], 1)

            def mix_channels3(k):
                j = k - 4
                pe.wait_ge(s["v3_ready"], j + 1)
                after(pe, "tpad_done", j)
                for c in range(2 * NP):
                    last = mm(p_t[:, c * C:(c + 1) * C], v3[:, c * HALF:(c + 1) * HALF], w("win3", 0, C),
                              start=True, stop=True)
                last.then_inc(s["t_done"], 1)

            def scan(k):
                j = k
                if isinstance(k, int) and k == 0:
                    pe.wait_ge(s["toep_ready"], 1)
                pe.wait_ge(s["seq_loaded"], 32 * (j + 1))
                pe.wait_ge(s["h_scaled_done"], j + 1)
                for m in range(2):
                    for mo in range(2):
                        for ci in range(2):
                            lhs = toep[:, m, ci, mo * 128:(mo + 1) * 128]
                            if m == 0:
                                dst = p_toep[:, mo * LN:(mo + 1) * LN]
                            else:
                                dst = p_toep[:, 2 * LN:4 * LN].rearrange("p (i a w) -> p a i w", i=NP, a=2)[:, mo]
                            last = mm(dst, lhs, seq[:, m, ci, :], start=ci == 0, stop=ci == 1)
                last.then_inc(s["toep_done"], 1)

            def output_product3(k):
                j = k - 5
                pe.wait_ge(s["prod3_done"], j + 1)
                after(pe, "x3_done", j + 3)
                mm(p_out[0:C, :], w("wout3", MID, CP), prod3[MID:CP, :], start=True, stop=True
                   ).then_inc(s["out_done"], 1)

            def block1_products(k):
                j = k - 1
                pe.wait_ge(s["v1_ready"], j + 1)
                after(pe, "tanh_gate_done", k + 1)
                mm(p_l1[0:C, :], w12[:, :], v1[:, :], start=True, stop=False)
                pe.wait_ge(s["max_done"], j + 1)
                mm(p_l1[0:C, :], w("w2", 0, C), max_all[:, :], start=False, stop=True).then_inc(s["l1_done"], 1)

            def to_spectrum(k):
                j = k - 4
                pe.wait_ge(s["t_pix_done"], j + 1)
                pe.wait_ge(s["gn_moments"], k)
                mm(p_spec[:, 0:2 * NP * C], w("dft"), t_pix[:, :, :].rearrange("p a b -> p (a b)"),
                   start=True, stop=True).then_inc(s["spec_done"], 1)

            def transpose_h1(k):
                j = k
                pe.wait_ge(s["h1_pix_done"], j + 1)
                after(pe, "gelu1_done", k - 1)
                for c in range(2 * NP):
                    last = nc.tensor.transpose(p_h1[0:GR, c * HALF:(c + 1) * HALF], h1_pix[:, c, :], w("ident"))
                last.then_inc(s["h1_back_done"], 1)

            def gate_product(k):
                j = k
                pe.wait_ge(s["h1_done"], j + 1)
                mm(p_gate[0:C, :], w("g2", 0, GR), h1[:, :], start=True, stop=True).then_inc(s["gate_done"], 1)

            def from_spectrum(k):
                j = k - 4
                pe.wait_ge(s["spec_ready"], j + 1)
                for c in range(2 * NP):
                    last = mm(p_inv[0:CP, c * HALF:(c + 1) * HALF], spec[:, c, :], w("idft"), start=True, stop=True)
                last.then_inc(s["inv_done"], 1)

            def convolve_first_halves(k):
                j = k - 3
                pe.wait_ge(s["xw_done"], j + 1)
                pe.wait_ge(s["xw_pool_done"], j + 1)
                convolution(0)

            def convolve_second_halves(k):
                convolution(1).then_inc(s["conv2_done"], 1)

            def change0_from_v(k):
                j = k
                pe.wait_ge(s["v0_ready"], j + 1)
                after(pe, "d_read", j)
                mm(p_d[0:C, :], dlhs[0:C, :], v0, start=True, stop=False).then_inc(s["d_from_v_done"], 1)

            def step(k, first):
                l0, l1, l2a, l2b, l3a, l3b = active(first)
                gn = gn_range(first)
                if l0 and first > 0:
                    first_norm_means(k)
                if l1:
                    change0_from_states(k - 1)
                if l2b:
                    convolve_first_halves(k)
                if l0:
                    project(k)
                if gn:
                    norm_means(k, gn)
                if l0:
                    mean_squares(k)
                if l2b:
                    convolve_second_halves(k)
                if l2a:
                    transpose_v2(k)
                if l3a:
                    mix_channels3(k)
                if l0:
                    transpose_h1(k)
                if l2b:
                    transpose_convolved(k)
                if l0:
                    scan(k)
                    gate_product(k)
                if l3a:
                    to_spectrum(k)
                if l0:
                    change0_from_v(k)
                if l3b:
                    output_product3(k)
                if l1:
                    block1_products(k)
                if l3a:
                    from_spectrum(k)

            def last_step(k):
                _, l1, l2a, l2b, l3a, l3b = active(k)
                gn = gn_range(k)
                if l2b:
                    convolve_first_halves(k)
                if l1:
                    change0_from_states(k - 1)
                if gn:
                    norm_means(k, gn)
                if l2b:
                    convolve_second_halves(k)
                if l3a:
                    mix_channels3(k)
                if l2a:
                    transpose_v2(k)
                if l2b:
                    transpose_convolved(k)
                if l3a:
                    to_spectrum(k)
                if l1:
                    block1_products(k)
                if l3a:
                    from_spectrum(k)
                if l3b:
                    output_product3(k)

            def convolution(co):
                for i, (n, ci) in enumerate([(n, ci) for n in range(NPT) for ci in range(2)]):
                    q = P8 * (1 + co - ci)
                    last = mm(p_conv[:, co * NP * C:(co + 1) * NP * C],
                              bumps[:, n, q:q + P8, :].rearrange("p a b -> p (a b)"),
                              xw[:, n, ci, :, :].rearrange("p a b -> p (a b)"),
                              start=i == 0, stop=i == 2 * NPT - 1)
                return last

            for k in range(FILL):
                step(k, k)
            with pe.Fori(FILL, PAIRS) as k:
                step(k, FILL)
            for k in range(PAIRS, STEPS):
                last_step(k)

        @block.scalar
        def _(act):
            f = nc.scalar.activation
            act.wait_ge(s["weights_in"], 16)
            f(sig_a[:, 0:1], w("alog", 0, 32), ACT.Tanh, scale=0.5).then_inc(s["setup_act"], 1)

            def place_row_states(k):
                j = k
                act.wait_ge(s["hs_loaded"], 48 * (j + 1))
                after(act, "d_done", j)
                f(v_hs[C:C + S, :].rearrange("p (i h w) -> p i h w", i=NP, h=H),
                  hs_row[C:C + S, :].rearrange("p (w i h) -> p i h w", i=NP, h=H), ACT.Copy
                  ).then_inc(s["hs_ready"], 1)

            def copy_convolved(k):
                j = k - 3
                act.wait_ge(s["conv2_done"], j + 1)
                after(act, "back_done", j)
                f(y_pix[:, :, :, :].rearrange("p a b c -> p (a b c)"), p_conv[:, 0:2 * NP * C], ACT.Copy
                  ).then_inc(s["y_pix_done"], 1)

            def normalise0(k):
                j = k
                act.wait_ge(s["gn0_shift"], j + 1)
                after(act, "d_from_v_done", j)
                after(act, "x0v0_done", j)
                for i in range(NP):
                    at = slice(i * PIX, (i + 1) * PIX)
                    last = f(v0[:, at], x0[:, at], ACT.Identity, bias=shift[:, 0, i:i + 1], scale=rstd[:, 0, i:i + 1])
                last.then_inc(s["v0_ready"], 1)

            def copy_change0(k):
                j = k
                act.wait_ge(s["d_done"], j + 1)
                after(act, "gated_done", j)
                f(d_half[:, :], p_d[0:C, :], ACT.Identity, bias=dbias[:, :]).then_inc(s["d_read"], 1)

            def square_v0(k):
                j = k
                act.wait_ge(s["v0_ready"], j + 1)
                after(act, "ssq_done", j)
                f(v0sq[:, :], v0, ACT.Square).then_inc(s["v0sq_done"], 1)

            def gates_and_inputs(k):
                j = k
                act.wait_ge(s["proj_done"], j + 1)
                after(act, "gu_done", j)
                hiw = "p (h i w) -> p i h w"
                f(tanh_g[:, :].rearrange(hiw, i=NP, w=W), img(p_proj, 32, 64), ACT.Tanh, bias=w("bg", 0, 32),
                  scale=0.5)
                f(u_half[:, :].rearrange(hiw, i=NP, w=W), img(p_proj, 0, 32), ACT.Identity, bias=w("bin", 0, 32)
                  ).then_inc(s["proj_read"], 1)

            def square_means(k):
                j = k
                act.wait_ge(s["ssq_done"], j + 1)
                after(act, "ln_var_done", j)
                f(ln_msq[:, :], p_h[:, :, GR], ACT.Square).then_inc(s["ln_msq_done"], 1)

            def order_rows(k):
                j = k
                act.wait_ge(s["gu_done"], j + 1)
                after(act, "seq_loaded", 32 * j)
                f(gu_row[0:S, :].rearrange("p (w i h) -> p i h w", i=NP, h=H),
                  gu_col[0:S, :].rearrange("p (h i w) -> p i h w", i=NP, w=W), ACT.Copy
                  ).then_inc(s["gu_row_done"], 1)

            def two_taps3(k):
                j = k - 5
                act.wait_ge(s["tpad_done"], j + 1)
                after(act, "two_taps_done", j)
                taps = w("wdw", 0, CP)
                f(tap_a[:, :, :], tpad[:, 0:ROWS, 0:W], ACT.Copy, scale=taps[:, 0:1])
                f(tap_b[:, :, :], tpad[:, 0:ROWS, 1:1 + W], ACT.Copy, scale=taps[:, 1:2]
                  ).then_inc(s["taps_ab_done"], 1)

            def normalise3(k):
                j = k - 4
                act.wait_ge(s["gn_shift"], k)
                after(act, "t_done", j)
                for i in range(NP):
                    at = slice(i * PIX, (i + 1) * PIX)
                    last = f(v3[:, at], x3[:, at], ACT.Identity, bias=shift[:, 3, i:i + 1], scale=rstd[:, 3, i:i + 1])
                last.then_inc(s["v3_ready"], 1)

            def gelu_h1(k):
                j = k
                act.wait_ge(s["h_in_done"], j + 1)
                after(act, "h1_back_done", j)
                f(h1_pix[:, :, :], h_in[:, :, :], ACT.Gelu).then_inc(s["h1_pix_done"], 1)

            def copy_v2_pixels(k):
                j = k - 2
                act.wait_ge(s["xt_done"], j + 1)
                after(act, "xw_done", j)
                after(act, "xw_pool_done", j)
                f(x_pix[:, :, :].rearrange("p a b -> p (a b)"), p_xt[:, 0:2 * NP * C], ACT.Copy
                  ).then_inc(s["x_pix_done"], 1)

            def copy_states(k):
                j = k
                act.wait_ge(s["toep_done"], j + 1)
                after(act, "hs_loaded", 48 * j)
                f(hs[:, :], p_toep[:, 0:4 * LN], ACT.Copy
                  ).then_inc(s["hs_read"], 1)

            def copy_t_pixels(k):
                j = k - 4
                act.wait_ge(s["t_done"], j + 1)
                after(act, "spec_done", j)
                f(t_pix[:, :, :].rearrange("p a b -> p (a b)"), p_t[:, 0:2 * NP * C], ACT.Copy
                  ).then_inc(s["t_pix_done"], 1)

            def gelu_gate3(k):
                j = k - 5
                act.wait_ge(s["tap_done"], 7 * (j + 1))
                after(act, "prod3_done", j)
                g = img(gelu3, MID, CP)
                for i in range(NP):
                    last = f(g[:, i, :, :], conv[0:HID2, i * HP:i * HP + H, :], ACT.Gelu)
                last.then_inc(s["gelu3_done"], 1)

            def keep_x3(k):
                j = k - 4
                act.wait_ge(s["x3_done"], j + 1)
                after(act, "x3_later_done", j)
                f(x3_late[:, :], x3[:, :], ACT.Copy).then_inc(s["x3_late_done"], 1)

            def gelu_block1(k):
                j = k - 1
                act.wait_ge(s["l1_done"], j + 1)
                after(act, "x2_done", j)
                f(gelu1[:, :], p_l1[0:C, :], ACT.Gelu, bias=bnb[:, :], scale=bns[:, :]).then_inc(s["gelu1_done"], 1)

            def keep_x2(k):
                j = k - 2
                act.wait_ge(s["x2_done"], j + 1)
                after(act, "x3_done", j)
                f(x2_late[:, :], x2[:, :], ACT.Copy).then_inc(s["x2_late_done"], 1)

            def pad_filtered(k):
                j = k - 4
                act.wait_ge(s["inv_done"], j + 1)
                after(act, "tap_done", 7 * j)
                f(tpad[:, 1:1 + NP * HP, 1:1 + W].rearrange("p (i h) w -> p i h w", i=NP)[:, :, 0:H, :],
                  img(p_inv, 0, CP), ACT.Copy).then_inc(s["tpad_done"], 1)

            def copy_h1(k):
                j = k
                act.wait_ge(s["h1_back_done"], j + 1)
                after(act, "gate_done", j)
                f(h1[:, :], p_h1[0:GR, :], ACT.Copy).then_inc(s["h1_done"], 1)

            def tanh_gate0(k):
                j = k
                act.wait_ge(s["gate_done"], j + 1)
                after(act, "gated_done", j)
                f(tanh_gate[:, :], p_gate[0:C, :], ACT.Tanh, bias=w("g2b", 0, C), scale=0.5
                  ).then_inc(s["tanh_gate_done"], 1)

            def hand_on_x3(k):
                j = k - 5
                act.wait_ge(s["x3_late_done"], j + 1)
                after(act, "x_out_done", j)
                f(x3_later[:, :], x3_late[:, :], ACT.Copy).then_inc(s["x3_later_done"], 1)

            def step(k, first):
                l0, l1, l2a, l2b, l3a, l3b = active(first)
                if l1:
                    place_row_states(k - 1)
                    copy_change0(k - 1)
                if l3b:
                    two_taps3(k)
                if l0:
                    normalise0(k)
                if l3b:
                    hand_on_x3(k)
                if l3a:
                    keep_x3(k)
                if l0:
                    square_v0(k)
                    gates_and_inputs(k)
                    square_means(k)
                    order_rows(k)
                if l3a:
                    normalise3(k)
                if l2b:
                    copy_convolved(k)
                if l0:
                    gelu_h1(k)
                    copy_h1(k)
                if l3b:
                    gelu_gate3(k)
                if l3a:
                    copy_t_pixels(k)
                if l2a:
                    copy_v2_pixels(k)
                if l0:
                    copy_states(k)
                    tanh_gate0(k)
                if l1:
                    gelu_block1(k)
                if l2a:
                    keep_x2(k)
                if l3a:
                    pad_filtered(k)

            def last_step(k):
                _, l1, l2a, l2b, l3a, l3b = active(k)
                if l1:
                    place_row_states(k - 1)
                if l3b:
                    two_taps3(k)
                if l1:
                    copy_change0(k - 1)
                if l3a:
                    normalise3(k)
                if l2b:
                    copy_convolved(k)
                if l3b:
                    hand_on_x3(k)
                if l3a:
                    keep_x3(k)
                    copy_t_pixels(k)
                if l2a:
                    copy_v2_pixels(k)
                if l3b:
                    gelu_gate3(k)
                if l2a:
                    keep_x2(k)
                if l1:
                    gelu_block1(k)
                if l3a:
                    pad_filtered(k)

            for k in range(FILL):
                step(k, k)
            with act.Fori(FILL, PAIRS) as k:
                step(k, FILL)
            for k in range(PAIRS, STEPS):
                last_step(k)

        @block.gpsimd
        def _(pool):
            tt = nc.gpsimd.tensor_tensor
            nc.gpsimd.memset(tpad[:, :, :], 0.0)
            nc.gpsimd.memset(spec[:, :, HID2:MID], 0.0).then_inc(s["setup_pool"], 1)
            pool.wait_ge(s["weights_in"], 16)
            nc.gpsimd.tensor_scalar(bnv[:, :], w("var", 0, C), BN_EPS, None, ALU.add).then_inc(s["setup_pool"], 1)
            pool.wait_ge(s["setup_pool"], 2)
            tt(bnr[:, :], bnv[:, :], w("mhalf", 0, C)[:, 0:1], ALU.pow).then_inc(s["setup_pool"], 1)

            def norm_factors(a, b, moments_done, neg, var, powered, shifted, n, free):
                q = "p a i -> p (a i)"
                m = (b - a) * NP
                pool.wait_ge(s[moments_done], n)
                free()
                tt(neg_mean[:, a:b, :].rearrange(q), moments[:, 0, a:b, :].rearrange(q), w("mone", 0, C)[:, 0:m],
                   ALU.mult).then_inc(s[neg], 1)
                pool.wait_ge(s[var], n)
                tt(rstd[:, a:b, :].rearrange(q), gvar[:, a:b, :].rearrange(q), w("mhalf", 0, C)[:, 0:m], ALU.pow
                   ).then_inc(s[powered], 1)
                pool.wait_ge(s[neg], n)
                pool.wait_ge(s[powered], n)
                tt(shift[:, a:b, :].rearrange(q), neg_mean[:, a:b, :].rearrange(q), rstd[:, a:b, :].rearrange(q),
                   ALU.mult).then_inc(s[shifted], 1)

            def first_norm_factors(k):
                norm_factors(0, 1, "gn0_moments", "gn0_neg", "gn0_var", "gn0_rstd", "gn0_shift", k + 1,
                             lambda: after(pool, "v0_ready", k))

            def layer_norm_factors(k):
                j = k
                pool.wait_ge(s["ln_var_done"], j + 1)
                after(pool, "h_scaled_done", j)
                tt(ln_rstd[:, :], ln_var[:, :], w("mhalf")[:, 0:2 * NP], ALU.pow
                   ).then_inc(s["ln_rstd_done"], 1)

            def add_two_taps(k):
                j = k - 5
                pool.wait_ge(s["taps_ab_done"], j + 1)
                after(pool, "tap_done", 7 * j)
                tt(two_taps[:, :, :], tap_a[:, :, :], tap_b[:, :, :], ALU.add).then_inc(s["two_taps_done"], 1)

            def later_norm_factors(k, gn):
                def free():
                    after(pool, "v1_ready", k - 1)
                    after(pool, "v2_ready", k - 2)
                    after(pool, "v3_ready", k - 4)
                norm_factors(*gn, "gn_moments", "gn_neg", "gn_var", "gn_rstd", "gn_shift", k, free)

            def add_v0(k):
                j = k
                pool.wait_ge(s["v0_ready"], j + 1)
                after(pool, "x1_done", j)
                tt(x0v0[:, :], x0[:, :], v0, ALU.add).then_inc(s["x0v0_done"], 1)

            def weigh_pixels(k):
                j = k - 2
                pool.wait_ge(s["x_pix_done"], j + 1)
                after(pool, "conv2_done", j)
                for n in XW_POOL:
                    last = tt(xw[:, n, :, :, :].rearrange("p a b c -> p (a b) c"), x_pix[:, :, :],
                              w("wb")[:, n * C:(n + 1) * C].unsqueeze(1).broadcast_to([128, 2 * NP, C]), ALU.mult)
                last.then_inc(s["xw_pool_done"], 1)

            def add_block1(k):
                j = k - 1
                pool.wait_ge(s["gelu1_done"], j + 1)
                pool.wait_ge(s["x1_done"], j + 1)
                after(pool, "v2_ready", j)
                after(pool, "x2_late_done", j)
                tt(x2[:, :], x1[:, :], gelu1[:, :], ALU.add).then_inc(s["x2_done"], 1)

            def add_block0(k):
                j = k
                pool.wait_ge(s["gated_done"], j + 1)
                pool.wait_ge(s["x0v0_done"], j + 1)
                after(pool, "v1_ready", j)
                after(pool, "x2_done", j)
                tt(x1[:, :], x0v0[:, :], gated[:, :], ALU.add).then_inc(s["x1_done"], 1)

            def step(k, first):
                l0, l1, l2a, l2b, l3a, l3b = active(first)
                gn = gn_range(first)
                if l0:
                    first_norm_factors(k)
                if l1:
                    add_block0(k - 1)
                if l3b:
                    add_two_taps(k)
                if l0:
                    add_v0(k)
                if gn:
                    later_norm_factors(k, gn)
                if l0:
                    layer_norm_factors(k)
                if l2a:
                    weigh_pixels(k)
                if l1:
                    add_block1(k)

            def last_step(k):
                _, l1, l2a, l2b, l3a, l3b = active(k)
                gn = gn_range(k)
                if l1:
                    add_block0(k - 1)
                if l3b:
                    add_two_taps(k)
                if gn:
                    later_norm_factors(k, gn)
                if l2a:
                    weigh_pixels(k)
                if l1:
                    add_block1(k)

            for k in range(FILL):
                step(k, k)
            with pool.Fori(FILL, PAIRS) as k:
                step(k, FILL)
            for k in range(PAIRS, STEPS):
                last_step(k)

        @block.vector
        def _(dve):
            tt, ts, stt = nc.vector.tensor_tensor, nc.vector.tensor_scalar, nc.vector.scalar_tensor_tensor
            copy = nc.vector.tensor_copy
            done = {}

            def link(ins, event="setup_steps"):
                done[event] = done.get(event, 0) + 1
                ins.then_inc(s[event], 1)
                dve.wait_ge(s[event], done[event])

            def half(t):
                return ts(t, t, 0.5, None, ALU.mult)

            def block_statistics(st):
                for i in range(NP):
                    last = nc.vector.bn_stats(stats[:, st, i, :], xs[st][:, i * PIX:(i + 1) * PIX])
                return last

            def statistics_end(a, b, events, n, taken=None):
                dve.wait_ge(s[events[0]], n if taken is None else taken)
                t = stats[:, a:b, :, :].rearrange("p a i (f t) -> p (a i f) t", f=2)
                q = "p a i f -> p (a i f)"
                tt(squares[:, a:b, :, :].rearrange(q), t[:, :, 1], t[:, :, 1], ALU.mult).then_inc(s[events[1]], 1)
                dve.wait_ge(s[events[1]], n)
                stt(halves[:, a:b, :, :].rearrange(q), t[:, :, 2], 2.0 / PIX, squares[:, a:b, :, :].rearrange(q),
                    ALU.mult, ALU.add).then_inc(s[events[2]], 1)

            def group_variance(a, b, events, n, p_gn=p_gn):
                m = (b - a) * NP
                dve.wait_ge(s[events[0]], n)
                nc.vector.tensor_reduce(moments[:, :, a:b, :], p_gn[0:C, 0:4 * m].rearrange(
                    "p (q a i f) -> p q a i f", q=2, a=b - a, i=NP), AX.X, ALU.add).then_inc(s[events[1]], 1)
                dve.wait_ge(s[events[1]], n)
                tt(msq[:, a:b, :], moments[:, 0, a:b, :], moments[:, 0, a:b, :], ALU.mult).then_inc(s[events[2]], 1)
                dve.wait_ge(s[events[2]], n)
                q = "p a i -> p (a i)"
                stt(gvar[:, a:b, :].rearrange(q), moments[:, 1, a:b, :].rearrange(q), GN_EPS,
                    msq[:, a:b, :].rearrange(q), ALU.add, ALU.subtract).then_inc(s[events[3]], 1)

            dve.wait_ge(s["weights_in"], 16)
            at = cols["proj"][0]
            half(wt[0:C, at:at + 32])
            half(w("bin", 0, 32))
            half(w("bg", 0, 32))
            half(w("g2b", 0, C))
            link(ts(gn1[:, :], w("g1", 0, C), w("nw", 0, C), None, ALU.mult), "gn1_done")
            dve.wait_ge(s["setup_act"], 1)
            link(ts(sig_a[:, 1:2], sig_a[:, 0:1], 0.5, 0.5, ALU.mult, ALU.add))
            dve.wait_ge(s["setup_pe"], 2)
            stt(pw_a[:, 0, :], w("id32", 0, 32), sig_a[:, 1:2], bank[0][0:32, 0:32], ALU.mult, ALU.add
                ).then_inc(s["powers_done"], 1)
            stt(pw_b[:, 0, :], w("id32", 0, 32), sig_a[:, 1:2], bank[1][0:32, 0:32], ALU.mult, ALU.add
                ).then_inc(s["powers_done"], 1)
            got = 2

            def powers(k):
                nonlocal got
                got += 2 if k < 8 else 1
                dve.wait_ge(s["setup_pe"], got)
                n = min(k, 15 - k)
                last = copy(pw_a[:, k:k + n, :].rearrange("p a b -> p (a b)"), bank[0][0:32, 0:n * 32])
                if k < 8:
                    last.then_inc(s["powers_done"], 1)
                    last = copy(pw_b[:, k:k + k, :].rearrange("p a b -> p (a b)"), bank[1][0:32, 0:k * 32])
                last.then_inc(s["powers_done"], 1)

            link(tt(dsum[:, :], w("skr", 0, C), w("skc", 0, C), ALU.add))
            powers(1)
            got += 1
            stt(dlhs[0:C, :], dsum[:, :], 0.25, w("halfid", 0, C), ALU.mult, ALU.subtract)
            ts(dlhs[C:128, :], dlhs[C:128, :], 0.125, None, ALU.mult)
            dve.wait_ge(s["x_loaded"], 16)
            block_statistics(0).then_inc(s["gn0_stats"], 1)
            statistics_end(0, 1, ("gn0_stats", "gn0_sq", "gn0_e2"), 1)
            powers(2)
            link(nc.vector.tensor_reduce(dbias[:, :], w("dbias", 0, C), AX.X, ALU.add))
            group_variance(0, 1, ("gn0_group", "gn0_moments", "gn0_msq", "gn0_var"), 1, bank[5])
            powers(4)
            ts(dbias[:, :], dbias[:, :], 0.25, None, ALU.mult)
            tt(w("ln", 0, C)[:, 0:GR], gn1[:, :], bank[2][0:C, 0:GR], ALU.subtract)
            tt(hbias[:, :], w("g1b"), bank[3][:, 0:GR], ALU.add)
            powers(8)
            dve.wait_ge(s["powers_done"], 9)
            tt(strip[:, 16:31, :], pw_a[:, :, 0:S], pw_a[:, :, S:2 * S], ALU.add)
            tt(strip[:, 14::-1, :], pw_a[:, :, 0:S], pw_a[:, :, S:2 * S], ALU.add)
            link(tt(strip[:, 15, :], w("id32", 0, 32)[:, 0:S], w("id32", 0, 32)[:, S:2 * S], ALU.add))
            ts(strip[:, 15, :], strip[:, 15, :], 2.0, None, ALU.mult
               ).then_inc(s["strip_done"], 1)
            copy(filt[:, :], bank[4][:, 0:C]).then_inc(s["setup_dve"], 1)

            def toeplitz():
                dve.wait_ge(s["lines_loaded"], 64)
                for m in range(2):
                    for half in range(2):
                        last = copy(toep[:, m, half, :].rearrange("p (a s b) -> p a s b", a=2, b=8),
                                    lines[:, m, half, :].rearrange("p (b a s) -> p a s b", a=2, b=8))
                last.then_inc(s["toep_ready"], 1)

            def later_weights():
                tt(w12[:, :], w("w1", 0, C), w("w2", 0, C), ALU.subtract)
                dve.wait_ge(s["setup_pool"], 3)
                tt(bnd[:, :], w("cb", 0, C), w("mean", 0, C), ALU.subtract)
                link(tt(bns[:, :], bnr[:, :], w("gamma", 0, C), ALU.mult))
                stt(bnb[:, :], bnd[:, :], bns[:, :], w("beta", 0, C), ALU.mult, ALU.add)
                link(nc.vector.reciprocal(rinv[:, :], w("rad")))
                link(ts(nrinv[:, :], rinv[:, :], -1.0, None, ALU.mult))
                wc = w("wc")
                for n in range(NPT):
                    ts(axd[:, n, :], w("dx"), wc[:, 2 * n:2 * n + 1], None, ALU.subtract)
                    last = ts(ayd[:, n, :], w("dy"), wc[:, 2 * n + 1:2 * n + 2], None, ALU.add)
                link(last)
                stt(axa[:, :, :], axd[:, :, :], -1.0, axd[:, :, :], ALU.mult, ALU.max)
                link(stt(aya[:, :, :], ayd[:, :, :], -1.0, ayd[:, :, :], ALU.mult, ALU.max))
                for n in range(NPT):
                    stt(ax[:, n, :], axa[:, n, :], rinv[:, n:n + 1], w("bigx"), ALU.mult, ALU.add)
                    last = stt(ay[:, n, :], aya[:, n, :], nrinv[:, n:n + 1], w("oney"), ALU.mult, ALU.add)
                link(last)
                for n in range(NPT):
                    last = tt(graw[:, n, :, :], ay[:, n, :].unsqueeze(2).broadcast_to([128, WIN, W]),
                              ax[:, n, :].unsqueeze(1).broadcast_to([128, WIN, W]), ALU.subtract)
                link(last)
                link(ts(bumps[:, :, :, :].rearrange("p a b c -> p (a b c)"),
                        graw[:, :, :, :].rearrange("p a b c -> p (a b c)"), 0.0, None, ALU.max))

            def normalise(st):
                for i in range(NP):
                    at = slice(i * PIX, (i + 1) * PIX)
                    last = ts(vs[st][:, at], xs[st][:, at], moments[:, 0, st, i:i + 1], rstd[:, st, i:i + 1],
                              ALU.subtract, ALU.mult)
                return last

            def taps3(k, first_tap, last_tap):
                j = k - 5
                if first_tap == 2:
                    dve.wait_ge(s["tpad_done"], j + 1)
                    dve.wait_ge(s["two_taps_done"], j + 1)
                    after(dve, "gelu3_done", j)
                    after(dve, "prod3_done", j)
                taps = w("wdw", 0, CP)
                for t in range(first_tap, last_tap):
                    src = tpad[:, t // 3:t // 3 + ROWS, t % 3:t % 3 + W]
                    so_far = two_taps if t == 2 else conv
                    if t > 2:
                        after(dve, "tap_done", 7 * j + t - 2)
                    stt(conv[:, :, :], src, taps[:, t:t + 1], so_far[:, :, :], ALU.mult, ALU.add
                        ).then_inc(s["tap_done"], 1)

            def blocks_counted(k):
                if isinstance(k, int):
                    return sum(min(max(k - age + 1, 0), PAIRS) for age in (1, 2, 4))
                return 3 * k - 4

            def first_norm_statistics(k):
                dve.wait_ge(s["x_loaded"], 16 * (k + 1))
                block_statistics(0).then_inc(s["gn0_stats"], 1)
                statistics_end(0, 1, ("gn0_stats", "gn0_sq", "gn0_e2"), k + 1)

            def first_norm_variance(k):
                group_variance(0, 1, ("gn0_group", "gn0_moments", "gn0_msq", "gn0_var"), k + 1)

            def gated_inputs(k):
                j = k
                dve.wait_ge(s["proj_read"], j + 1)
                after(dve, "gu_row_done", j)
                after(dve, "seq_loaded", 32 * j)
                stt(gu_col[:, :], tanh_g[:, :], 1.0, u_half[:, :], ALU.add, ALU.mult).then_inc(s["gu_done"], 1)

            def layer_norm_variance(k):
                j = k
                dve.wait_ge(s["ssq_done"], j + 1)
                dve.wait_ge(s["ln_msq_done"], j + 1)
                after(dve, "ln_rstd_done", j)
                stt(ln_var[:, :], p_ssq, LN_EPS, ln_msq[:, :], ALU.add, ALU.subtract
                    ).then_inc(s["ln_var_done"], 1)

            def later_norm_variance(k, gn):
                group_variance(*gn, ("gn_group", "gn_moments", "gn_msq", "gn_var"), k)

            def normalise1(k):
                j = k - 1
                dve.wait_ge(s["gn_rstd"], k)
                after(dve, "l1_done", j)
                after(dve, "horiz_done", j)
                normalise(1).then_inc(s["v1_ready"], 1)

            def normalise2(k):
                j = k - 2
                dve.wait_ge(s["gn_rstd"], k)
                after(dve, "xt_done", j)
                normalise(2).then_inc(s["v2_ready"], 1)

            def layer_norm_h1(k):
                j = k
                dve.wait_ge(s["ln_rstd_done"], j + 1)
                after(dve, "h1_pix_done", j)
                tt(h_scaled[:, :, :], p_h[:, :, 0:GR], ln_rstd[:, :].unsqueeze(2).broadcast_to([128, 2 * NP, GR]),
                   ALU.mult).then_inc(s["h_scaled_done"], 1)
                dve.wait_ge(s["h_scaled_done"], j + 1)
                tt(h_in[:, :, :], h_scaled[:, :, :], hbias[:, :].unsqueeze(1).broadcast_to([128, 2 * NP, GR]),
                   ALU.add).then_inc(s["h_in_done"], 1)

            def gate3(k):
                j = k - 5
                dve.wait_ge(s["gelu3_done"], j + 1)
                dve.wait_ge(s["tap_done"], 7 * (j + 1))
                after(dve, "out_done", j)
                g, p = img(gelu3, MID, CP), img(prod3, MID, CP)
                for i in range(NP):
                    last = tt(p[:, i, :, :], g[:, i, :, :], conv[MID:CP, i * HP:i * HP + H, :], ALU.mult)
                last.then_inc(s["prod3_done"], 1)

            def max_neighbours(k):
                j = k - 1
                dve.wait_ge(s["vert2_done"], j + 1)
                dve.wait_ge(s["horiz_done"], j + 1)
                after(dve, "l1_done", j)
                tt(max_all[:, :], max_v2[:, :], max_h[:, :], ALU.max).then_inc(s["max_done"], 1)

            def add_block3(k):
                j = k - 5
                dve.wait_ge(s["out_done"], j + 1)
                dve.wait_ge(s["x3_later_done"], j + 1)
                after(dve, "stored", 16 * j)
                tt(x_out[:, :], x3_later[:, :], p_out[0:C, :], ALU.add).then_inc(s["x_out_done"], 1)

            def weigh_pixels(k):
                j = k - 2
                dve.wait_ge(s["x_pix_done"], j + 1)
                after(dve, "conv2_done", j)
                for n in XW_DVE:
                    last = tt(xw[:, n, :, :, :].rearrange("p a b c -> p (a b) c"), x_pix[:, :, :],
                              w("wb")[:, n * C:(n + 1) * C].unsqueeze(1).broadcast_to([128, 2 * NP, C]), ALU.mult)
                last.then_inc(s["xw_done"], 1)

            def add_block2(k):
                j = k - 3
                dve.wait_ge(s["back_done"], j + 1)
                dve.wait_ge(s["x2_late_done"], j + 1)
                after(dve, "v3_ready", j)
                after(dve, "x3_late_done", j)
                tt(x3[:, :], x2_late[:, :], p_back[0:C, :], ALU.add).then_inc(s["x3_done"], 1)

            def filter_spectrum(k):
                j = k - 4
                dve.wait_ge(s["spec_done"], j + 1)
                after(dve, "inv_done", j)
                z = bass.AP(tensor=spec[:, :, :].tensor, offset=spec[:, :, :].offset,
                            ap=[list(spec[:, :, :].ap[0]), [CP, 2 * NP], [MID, 2], [1, HID2]])
                tt(z, p_spec[:, 0:2 * NP * C].rearrange("p (a b c) -> p a b c", b=2, c=HID2),
                   filt[:, :].rearrange("p (b c) -> p b c", b=2).unsqueeze(1).broadcast_to([128, 2 * NP, 2, HID2]),
                   ALU.mult).then_inc(s["spec_ready"], 1)

            def statistics3(k):
                after(dve, "x3_done", k - 3)
                block_statistics(3).then_inc(s["gn_stats"], 1)

            def statistics2(k):
                after(dve, "x2_done", k - 1)
                block_statistics(2).then_inc(s["gn_stats"], 1)

            def statistics1(k):
                after(dve, "x1_done", k)
                block_statistics(1).then_inc(s["gn_stats"], 1)

            def mean_squares_of_halves(k, gn):
                statistics_end(*gn, ("gn_stats", "gn_sq", "gn_e2"), k, blocks_counted(k))

            def gate0(k):
                j = k
                dve.wait_ge(s["tanh_gate_done"], j + 1)
                dve.wait_ge(s["d_read"], j + 1)
                after(dve, "x1_done", j)
                stt(gated[:, :], tanh_gate[:, :], 1.0, d_half[:, :], ALU.add, ALU.mult).then_inc(s["gated_done"], 1)

            def max_vertical_pairs(k):
                j = k - 1
                v, m1 = img(v1), img(max_v1)
                dve.wait_ge(s["v1_ready"], j + 1)
                after(dve, "max_done", j)
                tt(m1[:, :, 0:H - 2, :], v[:, :, 0:H - 2, :], v[:, :, 2:H, :], ALU.max)
                tt(m1[:, :, H - 2:H, :], v[:, :, H - 2:H, :], v[:, :, 0:2, :], ALU.max).then_inc(s["vert1_done"], 1)

            def max_horizontal(k):
                j = k - 1
                v, m = img(v1), img(max_h)
                tt(m[:, :, :, 2:W - 2], v[:, :, :, 0:W - 4], v[:, :, :, 4:W], ALU.max)
                tt(m[:, :, :, 0:2], v[:, :, :, W - 2:W], v[:, :, :, 2:4], ALU.max)
                tt(m[:, :, :, W - 2:W], v[:, :, :, W - 4:W - 2], v[:, :, :, 0:2], ALU.max
                   ).then_inc(s["horiz_done"], 1)

            def max_vertical(k):
                j = k - 1
                m1, m2 = img(max_v1), img(max_v2)
                dve.wait_ge(s["vert1_done"], j + 1)
                tt(m2[:, :, 2:H, :], m1[:, :, 2:H, :], m1[:, :, 0:H - 2, :], ALU.max)
                tt(m2[:, :, 0:2, :], m1[:, :, 0:2, :], m1[:, :, H - 2:H, :], ALU.max).then_inc(s["vert2_done"], 1)

            def step(k, first):
                l0, l1, l2a, l2b, l3a, l3b = active(first)
                gn = gn_range(first)
                if l3a:
                    statistics3(k)
                if l0 and first > 0:
                    first_norm_statistics(k)
                    first_norm_variance(k)
                if l2a:
                    statistics2(k)
                if l1:
                    gate0(k - 1)
                    statistics1(k)
                if l3b:
                    taps3(k, 2, 3)
                if gn:
                    mean_squares_of_halves(k, gn)
                if l3b:
                    taps3(k, 3, 5)
                if gn:
                    later_norm_variance(k, gn)
                if l0:
                    gated_inputs(k)
                    layer_norm_variance(k)
                if l3b:
                    taps3(k, 5, 6)
                if l2a:
                    normalise2(k)
                if l3b:
                    taps3(k, 6, 7)
                if l0:
                    layer_norm_h1(k)
                if l1:
                    normalise1(k)
                if l3b:
                    taps3(k, 7, 9)
                if l1:
                    max_vertical_pairs(k)
                if l2b:
                    add_block2(k)
                if l1:
                    max_horizontal(k)
                if l3b:
                    gate3(k)
                if l1:
                    max_vertical(k)
                    max_neighbours(k)
                if l3a:
                    filter_spectrum(k)
                if l3b:
                    add_block3(k)
                if l2a:
                    weigh_pixels(k)

            def last_step(k):
                _, l1, l2a, l2b, l3a, l3b = active(k)
                gn = gn_range(k)
                if l2a:
                    statistics2(k)
                if l3a:
                    statistics3(k)
                if l1:
                    gate0(k - 1)
                    statistics1(k)
                if gn:
                    mean_squares_of_halves(k, gn)
                if l3b:
                    taps3(k, 2, 3)
                if gn:
                    later_norm_variance(k, gn)
                if l3b:
                    taps3(k, 3, 6)
                if l2a:
                    normalise2(k)
                if l3b:
                    taps3(k, 6, 8)
                if l1:
                    normalise1(k)
                if l3b:
                    taps3(k, 8, 9)
                if l1:
                    max_vertical_pairs(k)
                if l2b:
                    add_block2(k)
                if l1:
                    max_horizontal(k)
                    max_vertical(k)
                    max_neighbours(k)
                if l3a:
                    filter_spectrum(k)
                if l3b:
                    gate3(k)
                if l2a:
                    weigh_pixels(k)
                if l3b:
                    add_block3(k)

            step(0, 0)
            toeplitz()
            later_weights()
            for k in range(1, FILL):
                step(k, k)
            with dve.Fori(FILL, PAIRS) as k:
                step(k, FILL)
            for k in range(PAIRS, STEPS):
                last_step(k)


def packed_weights(a):
    cols, n = weight_layout()
    wt = np.zeros((128, n), np.float32)

    def put(name, value, p0=0, c0=0):
        value = np.asarray(value)
        if value.ndim == 1:
            value = value[:, None]
        at = cols[name][0] + c0
        wt[p0:p0 + value.shape[0], at:at + value.shape[1]] = value

    for name, value in shape_constants().items():
        put(name, value)
    put("ln", np.full((C, 1), 1.0 / C), c0=GR)
    for i, d in enumerate(("row", "col")):
        g = {key: a[f"L0_conv_{d}_{key}"] for key in ("a_logit", "U", "V", "Win", "bin", "Wg", "bg", "Wout", "bout",
                                                      "Wskip", "bskip")}
        put("proj", g["Win"].T, c0=i * S)
        put("proj", g["Wg"].T, c0=32 + i * S)
        put("bin", g["bin"], p0=i * S)
        put("bg", g["bg"], p0=i * S)
        put("alog", g["a_logit"], p0=i * S)
        put("vt", g["V"].T, p0=i * R, c0=i * S)
        put("ut", g["U"].T, p0=i * R, c0=i * S)
        put("skr" if i == 0 else "skc", g["Wskip"].T)
        put("dlhs", g["Wout"].T, p0=C + i * S)
        put("dbias", g["bout"], c0=2 * i)
        put("dbias", g["bskip"], c0=2 * i + 1)
    put("g1", a["L0_conv_g1_w"].T)
    put("g1b", np.broadcast_to(a["L0_conv_g1_b"].reshape(1, GR), (128, GR)))
    put("nw", a["L0_conv_norm_w"])
    put("nb", a["L0_conv_norm_b"])
    put("g2", a["L0_conv_g2_w"].T)
    put("g2b", a["L0_conv_g2_b"])
    put("w1", a["L1_conv_conv_w"][:, :C].T)
    put("w2", a["L1_conv_conv_w"][:, C:].T)
    for name, key in (("cb", "conv_b"), ("gamma", "bn_gamma"), ("beta", "bn_beta"), ("mean", "bn_mean"),
                      ("var", "bn_var")):
        put(name, a["L1_conv_" + key])
    put("wc", np.broadcast_to(a["L2_conv_weight_coord"].reshape(1, 2 * NPT), (128, 2 * NPT)))
    put("rad", np.broadcast_to(a["L2_conv_radius"].reshape(1, NPT), (128, NPT)))
    put("wb", np.broadcast_to(a["L2_conv_weights"][0].T.reshape(1, NPT * C), (128, NPT * C)))
    put("filt", a["L3_conv_fft_filter"].reshape(C, NF).T)
    put("win3", a["L3_conv_w_in"].T)
    put("wout3", a["L3_conv_w_out"].T, p0=MID)
    taps = a["L3_conv_w_dw"].reshape(C, 9)
    put("wdw", taps[:HID2])
    put("wdw", taps[HID2:], p0=MID)
    return wt


def kernel(**inputs):
    import concourse.bacc as bacc
    from concourse.bass_utils import run_bass_kernel_spmd

    a = {name: np.asarray(value) for name, value in inputs.items()}
    nc = bacc.Bacc("TRN2", target_bir_lowering=False, num_devices=1)
    arrays = {
        "x_channels": np.ascontiguousarray(a["x"].transpose(1, 0, 2, 3).reshape(C, B * PIX)),
        "weights_packed": packed_weights(a),
    }
    args = [nc.dram_tensor(name, v.shape, mybir.dt.from_np(v.dtype), kind="ExternalInput").ap()
            for name, v in arrays.items()]
    out = nc.dram_tensor("out_channels", (C, B * PIX), mybir.dt.float32, kind="ExternalOutput").ap()
    build(nc, *args, out)
    got = run_bass_kernel_spmd(nc, [arrays], core_ids=[0]).results[0]["out_channels"]
    return np.ascontiguousarray(got.reshape(C, B, H, W).transpose(1, 0, 2, 3))
```
